# Optimizing a Trainium2 kernel written in Bass

```python
import numpy as np
import jax
import jax.numpy as jnp

def _softmax(x, axis=-1):
    return jax.nn.softmax(x, axis=axis)

def _gelu(x):
    return jax.nn.gelu(x, approximate=True)

def _silu(x):
    return jax.nn.silu(x)

def _sigmoid(x):
    return jax.nn.sigmoid(x)

def _layernorm(x, axis=-1, eps=1e-05):
    m = jnp.mean(x, axis=axis, keepdims=True)
    v = jnp.var(x, axis=axis, keepdims=True)
    return (x - m) / jnp.sqrt(v + eps)

def _scatter_add(tgt, idx, src, axis=0):
    return tgt.at[idx].add(src)

def _segment_sum(src, seg, n):
    return jax.ops.segment_sum(src, seg, n)
kernel_name = 'mk_adaln_d1_jaxref_r8_044678'

def setup_inputs(seed: int=0):
    np.random.seed(seed)
    _w = jnp.asarray

    def _L0_attn_setup():
        import jax, jax.numpy as jnp
        import numpy as np
        B, T, D, H = (4, 128, 128, 16)
        key = jax.random.key(seed)
        ks = jax.random.split(key, 7)
        x = jax.random.normal(ks[0], (B, T, D), dtype=jnp.float32)
        scale = 0.02
        Wq = jax.random.normal(ks[1], (D, D), dtype=jnp.float32) * scale
        Wk = jax.random.normal(ks[2], (D, D), dtype=jnp.float32) * scale
        Wv = jax.random.normal(ks[3], (D, D), dtype=jnp.float32) * scale
        bq = jax.random.normal(ks[4], (D,), dtype=jnp.float32) * scale
        bk = jax.random.normal(ks[5], (D,), dtype=jnp.float32) * scale
        bv = jax.random.normal(ks[6], (D,), dtype=jnp.float32) * scale
        temperature = jnp.ones((H, 1, 1), dtype=jnp.float32)
        return {'x': x, 'Wq': Wq, 'bq': bq, 'Wk': Wk, 'bk': bk, 'Wv': Wv, 'bv': bv, 'temperature': temperature}
    _L0_attn_in = _L0_attn_setup()

    def _L0_ffn_setup():
        import jax, jax.numpy as jnp
        import numpy as np
        DIM = 128
        DEPTH = 2
        HEADS = 8
        DIM_HEAD = 64
        WINDOW = 64
        INNER = HEADS * DIM_HEAD
        HID = int(DIM * 4 * 2 / 3)
        B, N = (2, 1024)
        QK_SCALE = 8.0

        def shift_token(t):
            t1, t2 = jnp.split(t, 2, axis=-1)
            t2 = jnp.pad(t2, ((0, 0), (1, 0), (0, 0)))[:, :-1]
            return jnp.concatenate([t1, t2], axis=-1)

        def l2norm(t):
            return t / jnp.clip(jnp.linalg.norm(t, axis=-1, keepdims=True), 1e-12)

        def rotate_half(x):
            x1, x2 = jnp.split(x, 2, axis=-1)
            return jnp.concatenate([-x2, x1], axis=-1)

        def rotary_xpos(q, k):
            n = q.shape[-2]
            half_idx = jnp.arange(0, DIM_HEAD, 2, dtype=jnp.float32)
            inv_freq = 1.0 / 10000.0 ** (half_idx / DIM_HEAD)
            t = jnp.arange(n, dtype=jnp.float32)
            freqs = t[:, None] * inv_freq[None, :]
            freqs = jnp.concatenate([freqs, freqs], axis=-1)
            base = (half_idx + 0.4 * DIM_HEAD) / (1.4 * DIM_HEAD)
            power = (t - n // 2) / float(WINDOW // 2)
            scale = base[None, :] ** power[:, None]
            scale = jnp.concatenate([scale, scale], axis=-1)
            cos, sin = (jnp.cos(freqs), jnp.sin(freqs))
            q = q * cos * scale + rotate_half(q) * sin * scale
            k = k * cos / scale + rotate_half(k) * sin / scale
            return (q, k)

        def local_attention(q, k, v):
            b, h, n, d = q.shape
            w = n // WINDOW
            bq = q.reshape(b, h, w, WINDOW, d) * QK_SCALE
            bk = k.reshape(b, h, w, WINDOW, d)
            bv = v.reshape(b, h, w, WINDOW, d)

            def look_around(t):
                p = jnp.pad(t, ((0, 0), (0, 0), (1, 0), (0, 0), (0, 0)))
                return jnp.concatenate([p[:, :, :w], p[:, :, 1:]], axis=3)
            bk, bv = (look_around(bk), look_around(bv))
            bt = jnp.arange(n).reshape(w, WINDOW)
            btp = jnp.pad(bt, ((1, 0), (0, 0)), constant_values=-1)
            btk = jnp.concatenate([btp[:w], btp[1:]], axis=1)
            sim = jnp.einsum('bhwid,bhwjd->bhwij', bq, bk)
            i = bt[:, :, None]
            j = btk[:, None, :]
            mask = (i < j) | (i > j + WINDOW) | (j == -1)
            sim = jnp.where(mask, -jnp.finfo(sim.dtype).max, sim)
            attn = jax.nn.softmax(sim, axis=-1)
            out = jnp.einsum('bhwij,bhwjd->bhwid', attn, bv)
            return out.reshape(b, h, n, d)

        def _layer(x, wqkv, qs, ksc, wo, lg, lb, w1, b1, w2, b2):
            b, n, _ = x.shape
            h = shift_token(x)
            qkv = h @ wqkv
            q, k, v = jnp.split(qkv, 3, axis=-1)
            to_heads = lambda t: t.reshape(b, n, HEADS, DIM_HEAD).transpose(0, 2, 1, 3)
            q, k, v = (to_heads(q), to_heads(k), to_heads(v))
            q = l2norm(q) * qs
            k = l2norm(k) * ksc
            q, k = rotary_xpos(q, k)
            o = local_attention(q, k, v)
            o = o.transpose(0, 2, 1, 3).reshape(b, n, INNER)
            x = x + o @ wo
            h = shift_token(x)
            mu = h.mean(-1, keepdims=True)
            var = h.var(-1, keepdims=True)
            h = (h - mu) / jnp.sqrt(var + 1e-05) * lg + lb
            h = h @ w1 + b1
            a, g = jnp.split(h, 2, axis=-1)
            h = a * jax.nn.gelu(g, approximate=False)
            x = x + h @ w2 + b2
            return x
        key = jax.random.key(seed)
        ks = jax.random.split(key, 6)
        return {'x': jax.random.normal(ks[0], (B, N, DIM), jnp.float32), 'wqkv': jax.random.normal(ks[1], (DEPTH, DIM, 3 * INNER), jnp.float32) * 0.02, 'q_scale': jnp.ones((DEPTH, DIM_HEAD), jnp.float32), 'k_scale': jnp.ones((DEPTH, DIM_HEAD), jnp.float32), 'wo': jax.random.normal(ks[2], (DEPTH, INNER, DIM), jnp.float32) * 0.02, 'ln_g': jnp.ones((DEPTH, DIM), jnp.float32), 'ln_b': jnp.zeros((DEPTH, DIM), jnp.float32), 'w1': jax.random.normal(ks[3], (DEPTH, DIM, 2 * HID), jnp.float32) * 0.02, 'b1': jnp.zeros((DEPTH, 2 * HID), jnp.float32), 'w2': jax.random.normal(ks[4], (DEPTH, HID, DIM), jnp.float32) * 0.02, 'b2': jnp.zeros((DEPTH, DIM), jnp.float32)}
    _L0_ffn_in = _L0_ffn_setup()
    _L0_c = _w((lambda *s: np.random.randn(*s).astype(np.float32) * 0.05)(8, 128))
    _L0_wmod = _w((lambda *s: np.random.randn(*s).astype(np.float32) * 0.05)(128, 6 * 128) * 128 ** (-0.5))
    _d = {'L0_attn_x': _L0_attn_in['x'], 'L0_attn_Wq': _L0_attn_in['Wq'], 'L0_attn_bq': _L0_attn_in['bq'], 'L0_attn_Wk': _L0_attn_in['Wk'], 'L0_attn_bk': _L0_attn_in['bk'], 'L0_attn_Wv': _L0_attn_in['Wv'], 'L0_attn_bv': _L0_attn_in['bv'], 'L0_attn_temperature': _L0_attn_in['temperature'], 'L0_ffn_wqkv': _L0_ffn_in['wqkv'], 'L0_ffn_q_scale': _L0_ffn_in['q_scale'], 'L0_ffn_k_scale': _L0_ffn_in['k_scale'], 'L0_ffn_wo': _L0_ffn_in['wo'], 'L0_ffn_ln_g': _L0_ffn_in['ln_g'], 'L0_ffn_ln_b': _L0_ffn_in['ln_b'], 'L0_ffn_w1': _L0_ffn_in['w1'], 'L0_ffn_b1': _L0_ffn_in['b1'], 'L0_ffn_w2': _L0_ffn_in['w2'], 'L0_ffn_b2': _L0_ffn_in['b2'], 'L0_c': _L0_c, 'L0_wmod': _L0_wmod}
    _x0 = _d['L0_attn_x']
    _d['L0_attn_x'] = jax.random.normal(jax.random.fold_in(jax.random.key(seed), 1), (8, 512, 128), dtype=_x0.dtype)
    del _x0
    return _d

def reference(L0_attn_x, L0_attn_Wq, L0_attn_bq, L0_attn_Wk, L0_attn_bk, L0_attn_Wv, L0_attn_bv, L0_attn_temperature, L0_ffn_wqkv, L0_ffn_q_scale, L0_ffn_k_scale, L0_ffn_wo, L0_ffn_ln_g, L0_ffn_ln_b, L0_ffn_w1, L0_ffn_b1, L0_ffn_w2, L0_ffn_b2, L0_c, L0_wmod):

    def _L0_attn_ref(x, Wq, bq, Wk, bk, Wv, bv, temperature):
        import jax, jax.numpy as jnp
        import numpy as np
        B, T, D, H = (4, 128, 128, 16)
        b, t, d = x.shape
        h = temperature.shape[0]
        dh = d // h
        q = (x @ Wq + bq).reshape(b, h, dh, t)
        k = (x @ Wk + bk).reshape(b, h, dh, t)
        v = (x @ Wv + bv).reshape(b, h, dh, t)
        attn = jnp.einsum('bhdt,bhds->bhts', k, v) * temperature
        attn = jax.nn.softmax(attn, axis=-1)
        out = jnp.einsum('bhdt,bhts->bhds', q, attn)
        return out.reshape(b, t, d)

    def _L0_ffn_ref(x, wqkv, q_scale, k_scale, wo, ln_g, ln_b, w1, b1, w2, b2):
        import jax, jax.numpy as jnp
        import numpy as np
        DIM = 128
        DEPTH = 2
        HEADS = 8
        DIM_HEAD = 64
        WINDOW = 64
        INNER = HEADS * DIM_HEAD
        HID = int(DIM * 4 * 2 / 3)
        B, N = (2, 1024)
        QK_SCALE = 8.0

        def shift_token(t):
            t1, t2 = jnp.split(t, 2, axis=-1)
            t2 = jnp.pad(t2, ((0, 0), (1, 0), (0, 0)))[:, :-1]
            return jnp.concatenate([t1, t2], axis=-1)

        def l2norm(t):
            return t / jnp.clip(jnp.linalg.norm(t, axis=-1, keepdims=True), 1e-12)

        def rotate_half(x):
            x1, x2 = jnp.split(x, 2, axis=-1)
            return jnp.concatenate([-x2, x1], axis=-1)

        def rotary_xpos(q, k):
            n = q.shape[-2]
            half_idx = jnp.arange(0, DIM_HEAD, 2, dtype=jnp.float32)
            inv_freq = 1.0 / 10000.0 ** (half_idx / DIM_HEAD)
            t = jnp.arange(n, dtype=jnp.float32)
            freqs = t[:, None] * inv_freq[None, :]
            freqs = jnp.concatenate([freqs, freqs], axis=-1)
            base = (half_idx + 0.4 * DIM_HEAD) / (1.4 * DIM_HEAD)
            power = (t - n // 2) / float(WINDOW // 2)
            scale = base[None, :] ** power[:, None]
            scale = jnp.concatenate([scale, scale], axis=-1)
            cos, sin = (jnp.cos(freqs), jnp.sin(freqs))
            q = q * cos * scale + rotate_half(q) * sin * scale
            k = k * cos / scale + rotate_half(k) * sin / scale
            return (q, k)

        def local_attention(q, k, v):
            b, h, n, d = q.shape
            w = n // WINDOW
            bq = q.reshape(b, h, w, WINDOW, d) * QK_SCALE
            bk = k.reshape(b, h, w, WINDOW, d)
            bv = v.reshape(b, h, w, WINDOW, d)

            def look_around(t):
                p = jnp.pad(t, ((0, 0), (0, 0), (1, 0), (0, 0), (0, 0)))
                return jnp.concatenate([p[:, :, :w], p[:, :, 1:]], axis=3)
            bk, bv = (look_around(bk), look_around(bv))
            bt = jnp.arange(n).reshape(w, WINDOW)
            btp = jnp.pad(bt, ((1, 0), (0, 0)), constant_values=-1)
            btk = jnp.concatenate([btp[:w], btp[1:]], axis=1)
            sim = jnp.einsum('bhwid,bhwjd->bhwij', bq, bk)
            i = bt[:, :, None]
            j = btk[:, None, :]
            mask = (i < j) | (i > j + WINDOW) | (j == -1)
            sim = jnp.where(mask, -jnp.finfo(sim.dtype).max, sim)
            attn = jax.nn.softmax(sim, axis=-1)
            out = jnp.einsum('bhwij,bhwjd->bhwid', attn, bv)
            return out.reshape(b, h, n, d)

        def _layer(x, wqkv, qs, ksc, wo, lg, lb, w1, b1, w2, b2):
            b, n, _ = x.shape
            h = shift_token(x)
            qkv = h @ wqkv
            q, k, v = jnp.split(qkv, 3, axis=-1)
            to_heads = lambda t: t.reshape(b, n, HEADS, DIM_HEAD).transpose(0, 2, 1, 3)
            q, k, v = (to_heads(q), to_heads(k), to_heads(v))
            q = l2norm(q) * qs
            k = l2norm(k) * ksc
            q, k = rotary_xpos(q, k)
            o = local_attention(q, k, v)
            o = o.transpose(0, 2, 1, 3).reshape(b, n, INNER)
            x = x + o @ wo
            h = shift_token(x)
            mu = h.mean(-1, keepdims=True)
            var = h.var(-1, keepdims=True)
            h = (h - mu) / jnp.sqrt(var + 1e-05) * lg + lb
            h = h @ w1 + b1
            a, g = jnp.split(h, 2, axis=-1)
            h = a * jax.nn.gelu(g, approximate=False)
            x = x + h @ w2 + b2
            return x
        for l in range(DEPTH):
            x = _layer(x, wqkv[l], q_scale[l], k_scale[l], wo[l], ln_g[l], ln_b[l], w1[l], b1[l], w2[l], b2[l])
        return x
    x = L0_attn_x
    mod = (_silu(L0_c) @ L0_wmod).reshape(L0_c.shape[0], 6, 1, -1)
    sa, ca, ga, sb, cb, gb = (mod[:, 0], mod[:, 1], mod[:, 2], mod[:, 3], mod[:, 4], mod[:, 5])
    ga = (2 * (ga >= 0) - 1) * jnp.maximum(jnp.abs(ga), 0.25)
    gb = (2 * (gb >= 0) - 1) * jnp.maximum(jnp.abs(gb), 0.25)
    h = _layernorm(x, axis=-1) * (1 + ca) + sa
    x = x + ga * _L0_attn_ref(h, L0_attn_Wq, L0_attn_bq, L0_attn_Wk, L0_attn_bk, L0_attn_Wv, L0_attn_bv, L0_attn_temperature)
    h = _layernorm(x, axis=-1) * (1 + cb) + sb
    x = x + gb * _L0_ffn_ref(h, L0_ffn_wqkv, L0_ffn_q_scale, L0_ffn_k_scale, L0_ffn_wo, L0_ffn_ln_g, L0_ffn_ln_b, L0_ffn_w1, L0_ffn_b1, L0_ffn_w2, L0_ffn_b2)
    return x

_drawn_inputs = setup_inputs


def setup_inputs(seed=0):
    import zlib

    import numpy as np

    out = dict(_drawn_inputs(seed))
    spreads = {'L0_attn_temperature': (1.0, 0.6),
     'L0_ffn_q_scale': (1.0, 0.6),
     'L0_ffn_k_scale': (1.0, 0.6),
     'L0_ffn_ln_g': (1.0, 0.6),
     'L0_ffn_ln_b': (0.0, 0.8),
     'L0_ffn_b1': (0.0, 0.8),
     'L0_ffn_b2': (0.0, 0.736)}
    factors = {'L0_attn_Wq': 8.0,
     'L0_attn_bq': 8.0,
     'L0_attn_Wk': 8.0,
     'L0_attn_bk': 8.0,
     'L0_attn_Wv': 8.0,
     'L0_attn_bv': 8.0,
     'L0_ffn_wqkv': 7.675,
     'L0_ffn_wo': 7.663,
     'L0_ffn_w1': 8.0,
     'L0_ffn_w2': 8.0}
    for name, (base, spread) in spreads.items():
        noise = np.random.default_rng([zlib.crc32(name.encode()), seed]).standard_normal(out[name].shape)
        drawn = base * np.exp(spread * noise) if base else spread * noise
        out[name] = jnp.asarray(drawn.astype(out[name].dtype))
    for name, factor in factors.items():
        out[name] = (out[name] * factor).astype(out[name].dtype)
    return out
```

```python
from contextlib import ExitStack

import numpy as np

import concourse.bass as bass
from concourse import mybir

F32 = mybir.dt.float32
F32R = mybir.dt.float32r
BF16 = mybir.dt.bfloat16
ALU = mybir.AluOpType
ACT = mybir.ActivationFunctionType
AX = mybir.AxisListType

P = 128
B, T, D = 8, 512, 128
J = T // P
HA, DA = 16, 8
HQ = 4
L = 2
H, DH, W = 8, 64, 64
INNER = H * DH
PAIRS = H // 2
NW = T // W
HID = (D * 4 * 2) // 3
CH = [P, P, HID - 2 * P]
LN_EPS = 1e-5
NORM_MIN2 = 1e-24
SHIFT2 = 2.0 ** 20
MASKED = -3.0e38

A_BANKS = 4
A_UNITS = [(hh, j, q) for hh in range(HQ) for j in range(J) for q in range(HQ)]
A_ORDER = ["xT", "qT", "k", "v"] + A_UNITS
A_USE = {s: i for i, s in enumerate(A_ORDER)}
A_PER = len(A_ORDER) // A_BANKS
B_BANKS = 3
AT_UNITS = [(p, g) for p in range(PAIRS) for g in range(2)]
NU = len(AT_UNITS)


def b_order():
    out = [("x2T", 0), ("x2T", 1)]
    for l in range(L):
        for i in range(J):
            out += [("q", l, i), ("k", l, i)]
        for i in range(J):
            out += [("qT", l, i), ("kT", l, i)]
        out += [("v", l, i) for i in range(J)]
        for n in range(len(AT_UNITS) + 2):
            if n < len(AT_UNITS):
                out.append(("sim", l, n))
            if 1 <= n <= len(AT_UNITS):
                out.append(("pT", l, n - 1))
            if n >= 2:
                out.append(("av", l, n - 2))
        out += [("wo", l), ("tok", l), ("lnT", l)]
        for c in range(3):
            out += [("gate", l, c), ("up", l, c)]
        out.append(("w2", l))
    return out + [("yT",)]


B_ORDER = b_order()
B_USE = {s: i for i, s in enumerate(B_ORDER)}
assert len(A_ORDER) % A_BANKS == 0 and len(B_ORDER) % B_BANKS == 0
B_PER = len(B_ORDER) // B_BANKS
GROUPS = [(hh, j) for hh in range(HQ) for j in range(J)]
E_RING = 3
N_W = 6
N_COLS = 2 + 3 * L + 6 * L + B
A_CHAIN = 2 + 3 + 2 + len(GROUPS)
B_CHAIN = (2 + 3) * (1 + L) + 3 * L


def build(nc, x, wmod, wqkv1, wqkv, wo, w1, w2, cols_in, rows_in_, rotary, out):
    with ExitStack() as ctx:
        def sb(name, shape, dt=F32):
            return ctx.enter_context(nc.sbuf_tensor(name, shape, dt))

        def sem(name):
            return ctx.enter_context(nc.semaphore(name))

        wqkv1_sb = sb("wqkv1_sb", [D, 3, D])
        wq_sb, wk_sb, wv_sb = (wqkv1_sb[:, n, :] for n in range(3))
        wqkv_sb = sb("wqkv_sb", [D, L, 3 * INNER])
        wo_sb = sb("wo_sb", [P, L, PAIRS, D])
        w1_sb = sb("w1_sb", [D, L, 2 * HID])
        w2_sb = sb("w2_sb", [P, L, 3, D])
        cols = sb("cols", [P, N_COLS])
        bq_col, temp_col = cols[:, 0:1], cols[:, 1:2]
        b2_col, lng_col, lnb_col = ([cols[:, 2 + n * L + l:3 + n * L + l] for l in range(L)] for n in range(3))
        b1_col = [[[cols[0:CH[k], n:n + 1] for k in range(3) for n in [2 + 3 * L + (l * 2 + a) * 3 + k]]
                   for a in range(2)] for l in range(L)]
        c_col = cols[:, N_COLS - B:N_COLS]
        rows = sb("rows", [P, 2 * D + 2 * L * DH])
        bk_bc, bv_bc = rows[:, 0:D], rows[:, D:2 * D]
        scale_bc = rows[:, 2 * D:].rearrange("p (w l d) -> p l w d", w=2, l=L)
        rot = sb("rot", [P, L, J, 2, 2, DH])
        gate_bc = sb("gate_bc", [P, 2, B, D])
        mod_col = sb("mod_col", [D, B, 4])
        cT = sb("cT", [D, 3, B])
        ident = sb("ident", [P, P])
        ident_h = sb("ident_h", [P, P], BF16)
        mask = sb("mask", [P, 8 * 2 * W], BF16)

        x_sb = sb("x_sb", [P, 2, J, D])
        stats, mv = sb("stats", [P, J, 6]), sb("mv", [P, J, 2])
        var_e, logs, rstd0, tmp4 = (sb(n, [P, J]) for n in ("var_e", "logs", "rstd0", "tmp4"))
        qT = sb("qT", [D, J, P])
        hi, lo = sb("hi", [P, 2, J, D], F32R), sb("lo", [P, 2, J, D], F32R)
        k_rows = sb("k_rows", [P, HQ, HQ, T], F32R)
        v_rows = sb("v_rows", [P, HQ, T], F32R)
        neg_max = sb("neg_max", [P, len(A_UNITS)])
        z = sb("z", [P, len(A_UNITS)])
        rz = sb("rz", [P, len(A_UNITS)])
        E = sb("E", [P, E_RING, HQ, T])
        kf = E[:, 0, 0:2, :].rearrange("p n (j f) -> p n j f", j=J)
        hT = E[:, 0, 2, :].rearrange("p (j n) -> p j n", j=J)
        xn = E[:, 0, 3, :].rearrange("p (j f) -> p j f", j=J)
        qz = sb("qz", [P, HQ, J, HQ, 32])

        xn2 = sb("xn2", [P, J, D])
        stats2, mv2 = sb("stats2", [P, J, 6]), sb("mv2", [P, J, 2])
        var2, logs2, rstd02, tmp2 = (sb(n, [P, J]) for n in ("var2", "logs2", "rstd02", "tmp2"))
        y = sb("y", [D, T])
        hs = sb("hs", [D, T])
        sq = sb("sq", [P, 2, INNER])
        sinp = sb("sinp", [P, 2, INNER])
        work = sb("work", [P, 2 * J * INNER])
        qk = work[:, :].rearrange("p (i w n) -> p i w n", i=J, w=2)
        v_al = work[:, 0:J * INNER].rearrange("p (i n) -> p i n", i=J)
        v_sh = work[:, J * INNER:].rearrange("p (i n) -> p i n", i=J)
        hn = work[:, 0:T].rearrange("p (i n) -> p i n", i=J)
        h2T = work[:, T:2 * T]
        gel = [work[:, (2 + n) * T:(3 + n) * T] for n in range(2)]
        up = [work[:, (4 + n) * T:(5 + n) * T] for n in range(3)]
        ss, rn, nt, nlog = (sb(n, [P, J, 2, H]) for n in ("ss", "rn", "nt", "nlog"))
        kT = sb("kT", [P, PAIRS, W + T])
        q_bd = sb("q_bd", [P, PAIRS, NW, 2, W])
        neg2, z2, rz2 = (sb(n, [P, len(AT_UNITS), 4]) for n in ("neg2", "z2", "rz2"))
        pr = sb("pr", [P, 2, 4, 2 * W])
        prT = sb("prT", [P, 2, 4, P])
        oT = sb("oT", [P, PAIRS, T])
        gated = hn
        wmod_sb = work[:, 0:6 * D]

        banks = [ctx.enter_context(nc.psum_tensor(f"bank{n}", [P, 512], F32)) for n in range(8)]
        O_BANK = banks[4]
        k_scr = nc.dram_tensor("k_scr", (HQ, HQ, 4, DA, T), F32)
        v_scr = nc.dram_tensor("v_scr", (HQ, HQ, 4, DA, T), F32)

        s_c, s_w, s_rot = sem("s_c"), sem("s_w"), sem("s_rot")
        s_zero, s_ident, s_mask = sem("s_zero"), sem("s_ident"), sem("s_mask")
        s_mask_done, s_mask_both = sem("s_mask_done"), sem("s_mask_both")
        s_silexp, s_sil, s_mod, s_setup = sem("s_silexp"), sem("s_sil"), sem("s_mod"), sem("s_setup")
        s_chain = sem("s_chain")
        x_loaded = sem("x_loaded")
        a_full = [sem(f"a_full{n}") for n in range(A_BANKS)]
        a_free = [sem(f"a_free{n}") for n in range(A_BANKS)]
        a_chain = sem("a_chain")
        a_var, a_log, a_rstd = sem("a_var"), sem("a_log"), sem("a_rstd")
        xn_ready = sem("xn_ready")
        parts_ready = sem("parts_ready")
        parts_out = sem("parts_out")
        rows_in = sem("rows_in")
        max_ready = sem("max_ready")
        qz_ready = sem("qz_ready")
        av_done = sem("av_done")
        o_read = sem("o_read")
        x2_ready = sem("x2_ready")
        b_full = [sem(f"b_full{n}") for n in range(B_BANKS)]
        b_free = [sem(f"b_free{n}") for n in range(B_BANKS)]
        b_chain = sem("b_chain")
        b_var, b_log, b_rstd = sem("b_var"), sem("b_log"), sem("b_rstd")
        xn2_ready = sem("xn2_ready")
        hs_low, hs_up = sem("hs_low"), sem("hs_up")
        sq_ready = sem("sq_ready")
        rot_sum = sem("rot_sum")
        ss_ready = sem("ss_ready")
        ss_all, ss_log, ss_rsqrt = sem("ss_all"), sem("ss_log"), sem("ss_rsqrt")
        qk_ready = sem("qk_ready")
        q_low = sem("q_low")
        v_pad = sem("v_pad")
        v_shifted = sem("v_shifted")
        max2 = sem("max2")
        rz2_ready = sem("rz2_ready")
        pr_ready = sem("pr_ready")
        out_ready = sem("out_ready")
        stored = sem("stored")

        def a_at(step):
            return A_USE[step] % A_BANKS, A_USE[step] // A_BANKS

        def b_at(step):
            return B_USE[step] % B_BANKS, B_USE[step] // B_BANKS

        credited = a_free + b_free + [rows_in, av_done, parts_out, o_read, stored, ss_ready, rot_sum]

        def passed(eng, s, n):
            eng.wait_ge(s, n + 1)

        def a_take(pe, b, step):
            k, n = a_at(step)
            passed(pe, a_free[k], b * A_PER + n)
            return banks[k], a_full[k]

        def a_see(eng, b, step):
            k, n = a_at(step)
            eng.wait_ge(a_full[k], b * A_PER + n + 1)
            return banks[k], a_free[k]

        def a_done(eng, b, step):
            k, n = a_at(step)
            passed(eng, a_free[k], b * A_PER + n + 1)

        def b_take(pe, b, step, *read):
            k, n = b_at(step)
            need = {k: n}
            for other in read:
                kk, m = b_at(other)
                need[kk] = max(need.get(kk, 0), m + 1)
            for kk, m in need.items():
                passed(pe, b_free[kk], b * B_PER + m)
            return banks[5 + k], b_full[k]

        def b_see(eng, b, step):
            k, n = b_at(step)
            eng.wait_ge(b_full[k], b * B_PER + n + 1)
            return banks[5 + k], b_free[k]

        def b_done(eng, b, *steps):
            need = {}
            for step in steps:
                k, n = b_at(step)
                need[k] = max(need.get(k, 0), n + 1)
            for k, n in need.items():
                passed(eng, b_free[k], b * B_PER + n)

        def stand(eng):
            eng.wait_ge(s_setup, 1)

        def y_done(eng, b, l, half):
            if half:
                b_done(eng, b, ("wo", l))
            elif l:
                b_done(eng, b, ("w2", l - 1))
            else:
                b_done(eng, b, ("x2T", 0), ("x2T", 1))

        block = ctx.enter_context(nc.Block())

        @block.sync
        def _(sp):
            def load(dst, src, s=s_w):
                sp.dma_start(dst, src).then_inc(s, 16)

            load(cols[:], cols_in, s_c)
            load(wmod_sb, wmod, s_c)
            load(wqkv1_sb[:], wqkv1)
            load(rows[:], rows_in_.partition_broadcast(P))
            load(wqkv_sb[:], wqkv)
            load(wo_sb[:], wo)
            load(w1_sb[:], w1)
            load(w2_sb[:], w2)
            for l in range(L):
                load(rot[:, l], rotary, s_rot)
            sp.wait_ge(s_mask_done, 1)
            load(mask[W:P], mask[0:W], s_mask_both)

            def a_load(b):
                stand(sp)
                passed(sp, stored, 16 * b)
                sp.dma_start(x_sb[:, b % 2], x[b].rearrange("(p j) f -> p j f", j=J)).then_inc(x_loaded, 16)

            def a_parts(b):
                passed(sp, rows_in, b * 16 * (HQ + 1))
                for n, (scr, parts) in enumerate(((k_scr, (hi, hi, lo, lo)), (v_scr, (hi, lo, hi, lo)))):
                    sp.wait_ge(parts_ready, b * 2 + n + 1)
                    for t, part in enumerate(parts):
                        sp.dma_start(scr[:, :, t].rearrange("q h d s -> (q h) d s"),
                                     part[:, n].rearrange("p j f -> p (j f)").bitcast(F32)).then_inc(parts_out, 16)
                passed(sp, parts_out, b * 16 * 8 + 16 * 8)
                passed(sp, av_done, b * len(GROUPS))
                for hh in range(HQ):
                    sp.dma_start(k_rows[32 * hh:32 * hh + 32, hh].bitcast(F32),
                                 k_scr[:, hh].rearrange("q t d s -> (t d) q s")).then_inc(rows_in, 16)
                sp.dma_start(v_rows[:].bitcast(F32), v_scr[:].rearrange("q h t d s -> (h t d) q s")).then_inc(rows_in, 16)

            def b_shift_v(b, l):
                b_done(sp, b, ("v", l, J - 1))
                sp.dma_start(v_sh[W:P, :, :], v_al[0:W, :, :]).then_inc(v_shifted, 16)
                sp.dma_start(v_sh[0:W, 1:J, :], v_al[W:P, 0:J - 1, :]).then_inc(v_shifted, 16)

            def b_store(b):
                sp.wait_ge(out_ready, b + 1)
                sp.dma_start(out[b].rearrange("(p j) f -> p j f", j=J), gated).then_inc(stored, 16)

            with sp.Fori(0, B) as b:
                a_load(b)
                a_parts(b)
                for l in range(L):
                    b_shift_v(b, l)
                b_store(b)
            passed(sp, stored, 16 * B)

        @block.gpsimd
        def _(pool):
            pool.memset(ident[:], 0.0).then_inc(s_zero, 1)
            pool.wait_ge(s_zero, 1)
            pool.affine_select(out=ident[:], in_=ident[:], compare_op=ALU.not_equal, fill=1.0, base=0,
                               pattern=[[-1, P]], channel_multiplier=1).then_inc(s_ident, 1)
            pool.wait_ge(s_ident, 1)
            pool.tensor_copy(ident_h[:], ident[:]).then_inc(s_ident, 1)
            pool.memset(mask[0:W], 0.0).then_inc(s_mask, 1)
            pool.wait_ge(s_mask, 1)
            pool.affine_select(out=mask[0:W], in_=mask[0:W], compare_op=ALU.is_ge, fill=MASKED, base=0,
                               pattern=[[0, 8], [1, 2 * W]], channel_multiplier=-1).then_inc(s_mask, 1)
            pool.wait_ge(s_mask, 2)
            pool.affine_select(out=mask[0:W], in_=mask[0:W], compare_op=ALU.is_ge, fill=MASKED, base=W,
                               pattern=[[0, 8], [-1, 2 * W]], channel_multiplier=1).then_inc(s_mask, 1)
            pool.wait_ge(s_mask, 3)
            pool.memset(mask[0:W, 0:W], MASKED).then_inc(s_mask_done, 1)
            pool.memset(k_rows[:].bitcast(F32), 0.0).then_inc(s_zero, 1)

            def b_rotary(b, l, n):
                i, w = divmod(n, 2)
                b_done(pool, b, ("qk"[w], l, i))
                pool.tensor_tensor(qk[:, i, w, :], qk[:, i, w, :], sinp[:, n % 2, :], ALU.add).then_inc(rot_sum, 1)

            def b_probs(b, l, u):
                pool.wait_ge(rz2_ready, (b * L + l) * NU + u + 1)
                pool.tensor_tensor(pr[:, u % 2], pr[:, u % 2],
                                   rz2[:, u, :].unsqueeze(2).broadcast_to([P, 4, 2 * W]),
                                   ALU.mult).then_inc(pr_ready, 1)

            with pool.Fori(0, B) as b:
                for l in range(L):
                    for n in range(2 * J):
                        b_rotary(b, l, n)
                    for u in range(NU):
                        b_probs(b, l, u)

        @block.scalar
        def _(act):
            act.wait_ge(s_c, 32)
            act.activation(cT[:, 1, :], c_col, ACT.Exp, scale=-1.0).then_inc(s_silexp, 1)
            act.wait_ge(s_setup, 1)
            act.wait_ge(s_w, 16 * N_W)

            def a_prep(b):
                act.wait_ge(a_var, b + 1)
                act.activation(logs[:], var_e[:], ACT.Ln).then_inc(a_log, 1)
                act.wait_ge(a_log, b + 1)
                act.activation(rstd0[:], logs[:], ACT.Exp, scale=-0.5).then_inc(a_rstd, 1)
                stand(act)
                bank, free = a_see(act, b, "xT")
                act.activation(hT, bank[:].rearrange("p (j n) -> p j n", j=J), ACT.Identity,
                               scale=mod_col[:, b, 0:1], bias=mod_col[:, b, 1:2]).then_inc(free, 1)
                bank, free = a_see(act, b, "qT")
                act.activation(qT[:], bank[:].rearrange("p (j n) -> p j n", j=J), ACT.Identity,
                               bias=bq_col).then_inc(free, 1)

            def a_exp(b, n):
                g, q = divmod(n, HQ)
                bank, free = a_see(act, b, A_UNITS[n])
                act.wait_ge(max_ready, b * len(A_UNITS) + n + 1)
                if q == 0:
                    passed(act, av_done, b * len(GROUPS) + max(g - E_RING + 1, 0))
                act.activation(E[:, g % E_RING, q, :], bank[:], ACT.Exp, bias=neg_max[:, n:n + 1],
                               accum_out=z[:, n:n + 1]).then_inc(free, 1)

            def b_rsqrt(b, n):
                act.wait_ge(b_var, b * (1 + L) + n + 1)
                act.activation(logs2[:], var2[:], ACT.Ln).then_inc(b_log, 1)
                act.wait_ge(b_log, b * (1 + L) + n + 1)
                act.activation(rstd02[:], logs2[:], ACT.Exp, scale=-0.5).then_inc(b_rstd, 1)

            def b_enter(b):
                b_rsqrt(b, 0)
                y_rows = y[:].rearrange("f (p j) -> f j p", j=J)
                for n in range(2):
                    stand(act)
                    bank, free = b_see(act, b, ("x2T", n))
                    act.activation(y_rows[:, 2 * n:2 * n + 2], bank[:, 0:2 * P].rearrange("p (j n) -> p j n", j=2),
                                   ACT.Identity, scale=mod_col[:, b, 2:3],
                                   bias=mod_col[:, b, 3:4]).then_inc(free, 1)

            def b_shift(b, l, half):
                y_done(act, b, l, half)
                act.activation(hs[0:W, :], y[0:W, :], ACT.Copy).then_inc(hs_low, 1)

            def b_square(b, l, n):
                i, w = divmod(n, 2)
                bank, _ = b_see(act, b, ("qk"[w], l, i))
                passed(act, ss_ready, (b * L + l) * 2 * J + max(n - 1, 0))
                act.activation(sq[:, n % 2], bank[:], ACT.Square).then_inc(sq_ready, 1)

            def b_norm(b, l):
                act.wait_ge(ss_all, b * L + l + 1)
                act.activation(nlog[:], ss[:], ACT.Ln).then_inc(ss_log, 1)
                act.wait_ge(ss_log, b * L + l + 1)
                act.activation(rn[:], nlog[:], ACT.Exp, scale=-0.5).then_inc(ss_rsqrt, 1)

            def b_heads(b, l, i):
                bank, _ = b_see(act, b, ("qT", l, i))
                act.activation(q_bd[0:W, :, 2 * i:2 * i + 2, 0, :],
                               bank[:].rearrange("p (c w t) -> p c w t", c=PAIRS, w=2)[0:W],
                               ACT.Copy).then_inc(q_low, 1)
                bank, free = b_see(act, b, ("kT", l, i))
                act.activation(kT[:, :, W + P * i:W + P * i + P], bank[:].rearrange("p (c t) -> p c t", c=PAIRS),
                               ACT.Copy).then_inc(free, 1)

            def b_values(b, l, i):
                bank, free = b_see(act, b, ("v", l, i))
                act.activation(v_al[:, i, :], bank[:], ACT.Copy).then_inc(free, 1)

            def b_exp(b, l, u):
                bank, free = b_see(act, b, ("sim", l, u))
                act.wait_ge(max2, (b * L + l) * NU + u + 1)
                if u >= 2:
                    b_see(act, b, ("pT", l, u - 2))
                for w in range(4):
                    last = act.activation(pr[:, u % 2, w, :], bank[:, 2 * W * w:2 * W * (w + 1)], ACT.Exp,
                                          bias=neg2[:, u, w:w + 1], accum_out=z2[:, u, w:w + 1])
                last.then_inc(free, 1)

            def b_probsT(b, l, u):
                bank, free = b_see(act, b, ("pT", l, u))
                if u >= 2:
                    b_see(act, b, ("av", l, u - 2))
                act.activation(prT[:, u % 2], bank[:].rearrange("p (w n) -> p w n", w=4), ACT.Copy).then_inc(free, 1)

            def b_ln(b, l):
                b_rsqrt(b, 1 + l)
                bank, free = b_see(act, b, ("lnT", l))
                act.activation(h2T, bank[:], ACT.Identity, scale=lng_col[l], bias=lnb_col[l]).then_inc(free, 1)

            def b_gelu(b, l, k):
                bank, free = b_see(act, b, ("gate", l, k))
                if k == 2:
                    b_done(act, b, ("up", l, 0))
                act.activation(gel[k % 2][0:CH[k]], bank[0:CH[k]], ACT.Gelu,
                               bias=b1_col[l][1][k]).then_inc(free, 1)

            with act.Fori(0, B) as b:
                a_prep(b)
                for n in range(len(A_UNITS)):
                    a_exp(b, n)
                b_enter(b)
                for l in range(L):
                    b_shift(b, l, 0)
                    for n in range(2 * J):
                        b_square(b, l, n)
                    b_norm(b, l)
                    for i in range(J):
                        b_heads(b, l, i)
                    for i in range(J):
                        b_values(b, l, i)
                    for u in range(NU + 1):
                        if u < NU:
                            b_exp(b, l, u)
                        if u >= 1:
                            b_probsT(b, l, u - 1)
                    b_shift(b, l, 1)
                    b_ln(b, l)
                    for k in range(3):
                        b_gelu(b, l, k)

        @block.vector
        def _(dve):
            def chained(s, per):
                state = [0, 0]

                def start(b):
                    state[:] = [b * per, 0]

                def link(ins):
                    state[1] += 1
                    ins.then_inc(s, 1)
                    dve.wait_ge(s, state[0] + state[1])

                def end():
                    assert state[1] == per, state
                return start, link, end

            s_start, s_link, _ = chained(s_chain, 0)
            a_start, a_link, a_end = chained(a_chain, A_CHAIN)
            b_start, b_link, b_end = chained(b_chain, B_CHAIN)

            for s in credited:
                dve.sem_inc(s, 1)
            s_start(0)
            s_link(dve.memset(qz[:], 0.0))
            s_link(dve.memset(q_bd[:], 0.0))
            s_link(dve.memset(kT[:, :, 0:W], 0.0))
            s_link(dve.memset(hs[W:P, 0:1], 0.0))
            dve.wait_ge(s_silexp, 1)
            s_link(dve.tensor_scalar(cT[:, 1, :], cT[:, 1, :], 1.0, None, ALU.add))
            s_link(dve.reciprocal(cT[:, 2, :], cT[:, 1, :]))
            dve.tensor_tensor(cT[:, 1, :], c_col, cT[:, 2, :], ALU.mult).then_inc(s_sil, 1)
            dve.wait_ge(s_mod, 1)
            m = banks[0][:, 0:4 * B].rearrange("p (m b) -> p m b", m=4)
            s_link(dve.tensor_scalar(mod_col[:, :, 0], m[:, 0], 1.0, None, ALU.add))
            s_link(dve.tensor_copy(mod_col[:, :, 1], m[:, 1]))
            s_link(dve.tensor_scalar(mod_col[:, :, 2], m[:, 2], 1.0, None, ALU.add))
            s_link(dve.tensor_copy(mod_col[:, :, 3], m[:, 3]))
            for n in range(4):
                s_link(dve.tensor_copy(gate_bc[:, :, 2 * n:2 * n + 2, :],
                                       banks[1 + n][:].rearrange("p (b g f) -> p g b f", b=2, g=2)))
            raw = gate_bc[:].rearrange("p g b f -> p (g b f)")
            sign, size = (E[:, n].rearrange("p q s -> p (q s)") for n in range(2))
            s_link(dve.tensor_scalar(sign, raw, 0.0, 2.0, ALU.is_ge, ALU.mult))
            s_link(dve.scalar_tensor_tensor(size, raw, -1.0, raw, ALU.mult, ALU.max))
            s_link(dve.tensor_scalar(size, size, 0.25, None, ALU.max))
            s_link(dve.scalar_tensor_tensor(raw, sign, -1.0, size, ALU.add, ALU.mult))
            dve.wait_ge(s_rot, 16 * L)
            dve.wait_ge(s_w, 16 * N_W)
            for l in range(L):
                for w in range(2):
                    sc = scale_bc[:, l, w, :]
                    s_link(dve.tensor_tensor(rot[:, l, :, w, 0, :], rot[:, l, :, w, 0, :],
                                             sc.unsqueeze(1).broadcast_to([P, J, DH]), ALU.mult))
                    for a in range(2):
                        r = rot[:, l, :, w, 1, 32 * a:32 * a + 32]
                        s_link(dve.tensor_tensor(r, r, sc[:, 32 - 32 * a:64 - 32 * a].unsqueeze(1)
                                                 .broadcast_to([P, J, 32]), ALU.mult))
            dve.wait_ge(s_zero, 2)
            dve.wait_ge(s_mask_both, 16)
            dve.tensor_scalar(bk_bc, bk_bc, temp_col, None, ALU.mult).then_inc(s_setup, 1)
            dve.wait_ge(s_setup, 1)

            def var_of(src, stats, mv, var, link, ready):
                for j in range(J):
                    last = dve.bn_stats(stats[:, j, :], src[:, j, :])
                link(last)
                dve.tensor_copy(var, ident[:, 0:J])
                for j in range(J):
                    last = dve.bn_aggr(mv[:, j, :], stats[:, j, :])
                link(last)
                dve.tensor_scalar(var, mv[:, :, 1], LN_EPS, None, ALU.add).then_inc(ready, 1)

            def newton(v, r, t, link):
                link(dve.scalar_tensor_tensor(t, v, -0.5, r, ALU.mult, ALU.mult))
                link(dve.tensor_tensor(t, t, r, ALU.mult))
                link(dve.scalar_tensor_tensor(r, t, 1.5, r, ALU.add, ALU.mult))

            def normalize(dst, src, mv, rstd):
                for j in range(J):
                    last = dve.tensor_scalar(dst[:, j, :], src[:, j, :], mv[:, j, 0:1], rstd[:, j:j + 1],
                                             ALU.subtract, ALU.mult)
                return last

            def a_ln(b):
                a_start(b)
                stand(dve)
                dve.wait_ge(x_loaded, 16 * b + 16)
                xb = x_sb[:, b % 2]
                var_of(xb, stats, mv, var_e[:], a_link, a_var)
                dve.wait_ge(a_rstd, b + 1)
                newton(var_e[:], rstd0[:], tmp4[:], a_link)
                normalize(xn, xb, mv, rstd0).then_inc(xn_ready, 1)

            def a_split(b):
                for n, step in enumerate("kv"):
                    bank, free = a_see(dve, b, step)
                    src = bank[:].rearrange("p (j f) -> p j f", j=J)
                    if n == 0:
                        passed(dve, parts_out, b * 16 * 8)
                        dve.scalar_tensor_tensor(kf[:, n], src, temp_col,
                                                 bk_bc.unsqueeze(1).broadcast_to([P, J, D]),
                                                 ALU.mult, ALU.add).then_inc(free, 1)
                    else:
                        dve.tensor_tensor(kf[:, n], src, bv_bc.unsqueeze(1).broadcast_to([P, J, D]),
                                          ALU.add).then_inc(free, 1)
                    a_done(dve, b, step)
                    a_link(dve.tensor_copy(hi[:, n], kf[:, n]))
                    dve.tensor_tensor(lo[:, n], kf[:, n], hi[:, n].bitcast(F32), ALU.subtract).then_inc(parts_ready, 1)

            def a_max(b, n):
                bank, _ = a_see(dve, b, A_UNITS[n])
                dve.tensor_reduce(neg_max[:, n:n + 1], bank[:], AX.X, ALU.max, negate=True).then_inc(max_ready, 1)

            def a_weigh(b, g):
                hh, j = GROUPS[g]
                a_done(dve, b, A_UNITS[HQ * g + HQ - 1])
                a_link(dve.reciprocal(rz[:, HQ * g:HQ * g + HQ], z[:, HQ * g:HQ * g + HQ]))
                if g == 0:
                    a_done(dve, b, "qT")
                dve.tensor_tensor(qz[:, hh, j, :, DA * hh:DA * hh + DA],
                                  qT[:, j, :].rearrange("p (q h d) -> p q h d", q=HQ, h=HQ)[:, :, hh, :],
                                  rz[:, HQ * g:HQ * g + HQ].unsqueeze(2).broadcast_to([P, HQ, DA]),
                                  ALU.mult).then_inc(qz_ready, 1)

            def a_residual(b):
                passed(dve, av_done, b * len(GROUPS) + len(GROUPS))
                dve.tensor_tensor(xn, O_BANK[:].rearrange("p (j f) -> p j f", j=J),
                                  gate_bc[:, 0, b, :].unsqueeze(1).broadcast_to([P, J, D]),
                                  ALU.mult).then_inc(o_read, 1)
                passed(dve, o_read, b + 1)
                xb = x_sb[:, b % 2]
                dve.tensor_tensor(xb, xb, xn, ALU.add).then_inc(x2_ready, 1)
                a_end()

            def b_enter(b):
                b_start(b)
                stand(dve)
                dve.wait_ge(x2_ready, b + 1)
                xb = x_sb[:, b % 2]
                var_of(xb, stats2, mv2, var2[:], b_link, b_var)
                dve.wait_ge(b_rstd, b * (1 + L) + 1)
                newton(var2[:], rstd02[:], tmp2[:], b_link)
                normalize(xn2, xb, mv2, rstd02).then_inc(xn2_ready, 1)

            def b_shift(b, l, half):
                y_done(dve, b, l, half)
                dve.tensor_copy(hs[W:P, 1:T], y[W:P, 0:T - 1]).then_inc(hs_up, 1)

            def b_rotate(b, l, n):
                i, w = divmod(n, 2)
                k = (b * L + l) * 2 * J + n
                dve.wait_ge(sq_ready, k + 1)
                bank, free = b_see(dve, b, ("qk"[w], l, i))
                dve.tensor_tensor(qk[:, i, w, :].rearrange("p (h d) -> p h d", h=H),
                                  bank[:].rearrange("p (h d) -> p h d", h=H),
                                  rot[:, l, i, w, 0, :].unsqueeze(1).broadcast_to([P, H, DH]), ALU.mult)
                passed(dve, rot_sum, (b * L + l) * 2 * J + max(n - 1, 0))
                dve.tensor_tensor(sinp[:, n % 2, :].rearrange("p (h a r) -> p h a r", h=H, a=2),
                                  bank[:].rearrange("p (h a r) -> p h a r", h=H, a=2)[:, :, ::-1, :],
                                  rot[:, l, i, w, 1, :].rearrange("p (a r) -> p a r", a=2).unsqueeze(1)
                                  .broadcast_to([P, H, 2, 32]), ALU.mult).then_inc(free, 1)
                dve.tensor_reduce(ss[:, i, w, :], sq[:, n % 2, :].rearrange("p (h d) -> p h d", h=H),
                                  AX.X, ALU.add).then_inc(ss_ready, 1)

            def b_norm(b, l):
                passed(dve, ss_ready, (b * L + l + 1) * 2 * J)
                dve.tensor_scalar(ss[:], ss[:], NORM_MIN2, SHIFT2, ALU.max, ALU.mult).then_inc(ss_all, 1)
                dve.wait_ge(ss_rsqrt, b * L + l + 1)
                newton(ss[:], rn[:], nt[:], b_link)
                for i in range(J):
                    passed(dve, rot_sum, (b * L + l) * 2 * J + 2 * i + 2)
                    v = qk[:, i].rearrange("p w (h d) -> p (w h) d", h=H)
                    dve.tensor_tensor(v, v, rn[:, i].rearrange("p w h -> p (w h)").unsqueeze(2)
                                      .broadcast_to([P, 2 * H, DH]), ALU.mult).then_inc(qk_ready, 1)

            def b_heads(b, l, i):
                bank, free = b_see(dve, b, ("qT", l, i))
                dve.wait_ge(q_low, (b * L + l) * J + i + 1)
                dve.tensor_copy(q_bd[W:P, :, 2 * i:2 * i + 2, 1, :],
                                bank[:].rearrange("p (c w t) -> p c w t", c=PAIRS, w=2)[W:P]).then_inc(free, 1)

            def b_pad_v(b, l):
                b_see(dve, b, ("v", l, 0))
                dve.memset(v_sh[0:W, 0, :], 0.0).then_inc(v_pad, 1)

            def b_max(b, l, u):
                bank, _ = b_see(dve, b, ("sim", l, u))
                dve.tensor_reduce(neg2[:, u, :], bank[:].rearrange("p (w n) -> p w n", w=4), AX.X, ALU.max,
                                  negate=True).then_inc(max2, 1)

            def b_sums(b, l, u):
                b_done(dve, b, ("sim", l, u))
                dve.reciprocal(rz2[:, u, :], z2[:, u, :]).then_inc(rz2_ready, 1)

            def b_heads_out(b, l, u):
                p, g = AT_UNITS[u]
                bank, free = b_see(dve, b, ("av", l, u))
                src = bank[:].rearrange("p (w h t) -> p w h t", w=4, h=2)
                dst = oT[:, p, 4 * W * g:4 * W * (g + 1)].rearrange("p (w t) -> p w t", w=4)
                dve.tensor_copy(dst[0:W], src[0:W, :, 0, :])
                dve.tensor_copy(dst[W:P], src[W:P, :, 1, :]).then_inc(free, 1)

            def b_residual(b, l):
                bank, free = b_see(dve, b, ("wo", l))
                y_read(dve, b, l, 0)
                dve.tensor_tensor(y[:], bank[:], y[:], ALU.add).then_inc(free, 1)

            def y_read(dve, b, l, half):
                dve.wait_ge(hs_low, (b * L + l) * 2 + half + 1)
                dve.wait_ge(hs_up, (b * L + l) * 2 + half + 1)

            def b_ln(b, l):
                stand(dve)
                bank, free = b_see(dve, b, ("tok", l))
                src = bank[:].rearrange("p (j f) -> p j f", j=J)
                var_of(src, stats2, mv2, var2[:], b_link, b_var)
                dve.wait_ge(b_rstd, b * (1 + L) + 2 + l)
                newton(var2[:], rstd02[:], tmp2[:], b_link)
                normalize(hn, src, mv2, rstd02).then_inc(free, 1)

            def b_up(b, l, k):
                bank, free = b_see(dve, b, ("up", l, k))
                b_done(dve, b, ("gate", l, k))
                dve.scalar_tensor_tensor(up[k][0:CH[k]], bank[0:CH[k]], b1_col[l][0][k],
                                         gel[k % 2][0:CH[k]], ALU.add, ALU.mult).then_inc(free, 1)

            def b_down(b, l):
                bank, free = b_see(dve, b, ("w2", l))
                y_read(dve, b, l, 1)
                dve.scalar_tensor_tensor(y[:], bank[:], b2_col[l], y[:], ALU.add, ALU.add).then_inc(free, 1)

            def b_out(b):
                bank, free = b_see(dve, b, ("yT",))
                passed(dve, stored, 16 * b)
                dve.tensor_tensor(gated, bank[:].rearrange("p (j f) -> p j f", j=J),
                                  gate_bc[:, 1, b, :].unsqueeze(1).broadcast_to([P, J, D]),
                                  ALU.mult).then_inc(free, 1)
                b_done(dve, b, ("yT",))
                dve.tensor_tensor(gated, gated, x_sb[:, b % 2], ALU.add).then_inc(out_ready, 1)
                b_end()

            with dve.Fori(0, B) as b:
                a_ln(b)
                a_split(b)
                for n in range(len(A_UNITS) + 2):
                    if n < len(A_UNITS):
                        a_max(b, n)
                    if n >= 5 and (n - 5) % HQ == 0:
                        a_weigh(b, (n - 5) // HQ)
                a_residual(b)
                b_enter(b)
                for l in range(L):
                    b_shift(b, l, 0)
                    for n in range(2 * J):
                        b_rotate(b, l, n)
                    b_norm(b, l)
                    for i in range(J):
                        b_heads(b, l, i)
                    b_pad_v(b, l)
                    for u in range(NU + 2):
                        if u < NU:
                            b_max(b, l, u)
                        if 1 <= u <= NU:
                            b_sums(b, l, u - 1)
                        if u >= 2:
                            b_heads_out(b, l, u - 2)
                    b_residual(b, l)
                    b_shift(b, l, 1)
                    b_ln(b, l)
                    for k in range(3):
                        b_up(b, l, k)
                    b_down(b, l)
                b_out(b)

        @block.tensor
        def _(pe):
            pe.wait_ge(s_c, 32)
            pe.wait_ge(s_sil, 1)
            sil = cT[:, 1, :]
            for n, m in enumerate((1, 0, 4, 3)):
                pe.matmul(banks[0][:, B * n:B * (n + 1)], wmod_sb[:, D * m:D * (m + 1)], sil, start=True, stop=True)
            for b in range(B):
                for n, m in enumerate((2, 5)):
                    o = (b % 2) * 2 * D + n * D
                    last = pe.matmul(banks[1 + b // 2][:, o:o + D], sil[:, b:b + 1].broadcast_to([D, P]),
                                     wmod_sb[:, D * m:D * (m + 1)], start=True, stop=True)
            last.then_inc(s_mod, 1)
            pe.wait_ge(s_setup, 1)
            pe.wait_ge(s_w, 16 * N_W)
            pe.wait_ge(s_ident, 2)

            def a_transpose(b):
                pe.wait_ge(xn_ready, b + 1)
                bank, full = a_take(pe, b, "xT")
                for j in range(J):
                    last = pe.transpose(bank[:, P * j:P * (j + 1)], xn[:, j, :], ident[:])
                last.then_inc(full, 1)

            def a_project(b):
                a_done(pe, b, "xT")
                bank, full = a_take(pe, b, "qT")
                pe.matmul(bank[:], wq_sb, E[:, 0, 2, :], start=True, stop=True).then_inc(full, 1)
                for step, w in (("k", wk_sb), ("v", wv_sb)):
                    bank, full = a_take(pe, b, step)
                    for j in range(J):
                        last = pe.matmul(bank[:, D * j:D * (j + 1)], hT[:, j, :], w, start=True, stop=True)
                    last.then_inc(full, 1)

            def a_scores(b, n):
                hh, j, q = A_UNITS[n]
                if n == 0:
                    passed(pe, rows_in, (b + 1) * 16 * (HQ + 1))
                bank, full = a_take(pe, b, A_UNITS[n])
                pe.matmul(bank[:], k_rows[:, hh, q, P * j:P * (j + 1)], v_rows[:, q, :],
                          start=True, stop=True).then_inc(full, 1)

            def a_values(b, g):
                hh, j = GROUPS[g]
                pe.wait_ge(qz_ready, b * len(GROUPS) + g + 1)
                if g == 0:
                    passed(pe, o_read, b)
                for q in range(HQ):
                    last = pe.matmul(O_BANK[32 * q:32 * q + 32, :], qz[:, hh, j, q, :], E[:, g % E_RING, q, :],
                                     start=(g == 0), stop=(g == len(GROUPS) - 1))
                last.then_inc(av_done, 1)

            def b_enter(b):
                pe.wait_ge(xn2_ready, b + 1)
                for n in range(2):
                    bank, full = b_take(pe, b, ("x2T", n))
                    for j in range(2):
                        last = pe.transpose(bank[:, P * j:P * (j + 1)], xn2[:, 2 * n + j, :], ident[:])
                    last.then_inc(full, 1)

            def hs_wait(b, l, half):
                pe.wait_ge(hs_low, (b * L + l) * 2 + half + 1)
                pe.wait_ge(hs_up, (b * L + l) * 2 + half + 1)

            def b_project(b, l, i, w):
                bank, full = b_take(pe, b, ("qkv"[w], l, i))
                pe.matmul(bank[:], hs[:, P * i:P * (i + 1)], wqkv_sb[:, l, INNER * w:INNER * (w + 1)],
                          start=True, stop=True).then_inc(full, 1)

            def b_heads(b, l, i):
                pe.wait_ge(qk_ready, (b * L + l) * J + i + 1)
                for w in range(2):
                    bank, full = b_take(pe, b, (("qT", "kT")[w], l, i))
                    for p in range(PAIRS):
                        last = pe.transpose(bank[:, P * p:P * (p + 1)], qk[:, i, w, P * p:P * (p + 1)], ident[:])
                    last.then_inc(full, 1)

            def b_scores(b, l, u):
                p, g = AT_UNITS[u]
                tiles = [(s, l, 2 * g + i) for s in ("qT", "kT") for i in range(2)] if u < 2 else []
                bank, full = b_take(pe, b, ("sim", l, u), *tiles)
                pe.matmul(bank[:], ident_h[:], mask[:, (1 if g else 0) * 512:(2 if g else 1) * 512],
                          start=True, stop=False)
                for w in range(4):
                    n = 4 * g + w
                    last = pe.matmul(bank[:, 2 * W * w:2 * W * (w + 1)], q_bd[:, p, n].rearrange("p h t -> p (h t)"),
                                     kT[:, p, W * n:W * n + 2 * W], start=False, stop=(w == 3))
                last.then_inc(full, 1)

            def b_probsT(b, l, u):
                pe.wait_ge(pr_ready, (b * L + l) * NU + u + 1)
                bank, full = b_take(pe, b, ("pT", l, u))
                for w in range(4):
                    last = pe.transpose(bank[:, P * w:P * (w + 1)], pr[:, u % 2, w, :], ident[:])
                last.then_inc(full, 1)

            def b_values(b, l, u):
                p, g = AT_UNITS[u]
                if u == 0:
                    pe.wait_ge(v_shifted, (b * L + l + 1) * 32)
                    pe.wait_ge(v_pad, b * L + l + 1)
                tiles = [("v", l, i) for i in range(J)] if u == 0 else []
                bank, full = b_take(pe, b, ("av", l, u), ("pT", l, u), *tiles)
                for w in range(4):
                    n = 4 * g + w
                    v = v_al[:, n // 2] if n % 2 else v_sh[:, n // 2]
                    last = pe.matmul(bank[:, P * w:P * (w + 1)], v[:, P * p:P * (p + 1)], prT[:, u % 2, w, :],
                                     start=True, stop=True)
                last.then_inc(full, 1)

            def b_project_out(b, l):
                bank, full = b_take(pe, b, ("wo", l), *(("av", l, u) for u in range(NU)))
                for p in range(PAIRS):
                    last = pe.matmul(bank[:], wo_sb[:, l, p, :], oT[:, p, :], start=(p == 0), stop=(p == PAIRS - 1))
                last.then_inc(full, 1)

            def b_ln(b, l):
                hs_wait(b, l, 1)
                bank, full = b_take(pe, b, ("tok", l))
                for i in range(J):
                    last = pe.transpose(bank[:, P * i:P * (i + 1)], hs[:, P * i:P * (i + 1)], ident[:])
                last.then_inc(full, 1)
                bank, full = b_take(pe, b, ("lnT", l), ("tok", l))
                for i in range(J):
                    last = pe.transpose(bank[:, P * i:P * (i + 1)], hn[:, i, :], ident[:])
                last.then_inc(full, 1)

            def b_hidden(b, l, k, a):
                bank, full = b_take(pe, b, (("up", "gate")[a], l, k), ("lnT", l))
                o = a * HID + P * k
                pe.matmul(bank[0:CH[k]], w1_sb[:, l, o:o + CH[k]], h2T, start=True, stop=True).then_inc(full, 1)

            def b_down(b, l):
                bank, full = b_take(pe, b, ("w2", l), *(("up", l, k) for k in range(3)))
                for k in range(3):
                    last = pe.matmul(bank[:], w2_sb[0:CH[k], l, k, :], up[k][0:CH[k]], start=(k == 0), stop=(k == 2))
                last.then_inc(full, 1)

            def b_leave(b):
                bank, full = b_take(pe, b, ("yT",), ("w2", L - 1))
                y_rows = y[:].rearrange("f (p j) -> f j p", j=J)
                for j in range(J):
                    last = pe.transpose(bank[:, P * j:P * (j + 1)], y_rows[:, j, :], ident[:])
                last.then_inc(full, 1)

            with pe.Fori(0, B) as b:
                a_transpose(b)
                a_project(b)
                for n in range(len(A_UNITS)):
                    a_scores(b, n)
                    if n >= 7 and (n - 7) % HQ == 0:
                        a_values(b, (n - 7) // HQ)
                a_values(b, len(GROUPS) - 1)
                b_enter(b)
                for l in range(L):
                    hs_wait(b, l, 0)
                    for i in range(J):
                        for w in range(2):
                            b_project(b, l, i, w)
                    for i in range(J):
                        b_heads(b, l, i)
                    for i in range(J):
                        b_project(b, l, i, 2)
                    for u in range(NU + 2):
                        if u < NU:
                            b_scores(b, l, u)
                        if 1 <= u <= NU:
                            b_probsT(b, l, u - 1)
                        if u >= 2:
                            b_values(b, l, u - 2)
                    b_project_out(b, l)
                    b_ln(b, l)
                    for k in range(3):
                        b_hidden(b, l, k, 1)
                        b_hidden(b, l, k, 0)
                    b_down(b, l)
                b_leave(b)


def laid_out(inputs):
    a = {n[3:]: np.asarray(v) for n, v in inputs.items()}
    cols = np.zeros((P, N_COLS), np.float32)
    cols[:, 0] = a["attn_bq"]
    cols[:, 1] = np.repeat(a["attn_temperature"].reshape(-1), DA)
    for l in range(L):
        cols[:, 2 + l] = a["ffn_b2"][l]
        cols[:, 2 + L + l] = a["ffn_ln_g"][l]
        cols[:, 2 + 2 * L + l] = a["ffn_ln_b"][l]
        for h in range(2):
            for k in range(3):
                cols[:CH[k], 2 + 3 * L + (l * 2 + h) * 3 + k] = a["ffn_b1"][l, h * HID + P * k:][:CH[k]]
    cols[:, N_COLS - B:] = a["c"].T
    w2 = np.zeros((L, 3 * P, D), np.float32)
    w2[:, :HID] = a["ffn_w2"]
    return {
        "x": a["attn_x"], "wmod": a["wmod"],
        "wqkv1": np.stack([a["attn_Wq"], a["attn_Wk"], a["attn_Wv"]], 1),
        "wqkv": a["ffn_wqkv"].transpose(1, 0, 2),
        "wo": a["ffn_wo"].reshape(L, PAIRS, P, D).transpose(2, 0, 1, 3),
        "w1": a["ffn_w1"].transpose(1, 0, 2),
        "w2": w2.reshape(L, 3, P, D).transpose(2, 0, 1, 3),
        "cols": cols,
        "rows": np.concatenate([a["attn_bk"], a["attn_bv"], a["ffn_q_scale"].reshape(-1), a["ffn_k_scale"].reshape(-1)]),
        "rotary": rotary_tables(),
    }


def rotary_tables():
    half = np.arange(0, DH, 2, dtype=np.float32)
    inv = (np.float32(1.0) / np.float32(10000.0) ** (half / np.float32(DH))).astype(np.float32)
    t = np.arange(T, dtype=np.float32)
    freqs = t[:, None] * inv[None, :]
    freqs = np.concatenate([freqs, freqs], -1).astype(np.float64)
    base = (half + np.float32(0.4 * DH)) / np.float32(1.4 * DH)
    power = (t - T // 2) / np.float32(W // 2)
    scale = base[None, :].astype(np.float32) ** power[:, None]
    scale = np.concatenate([scale, scale], -1).astype(np.float64)
    sign = np.where(np.arange(DH) < DH // 2, -1.0, 1.0)
    cos, sin = np.cos(freqs), np.sin(freqs) * sign
    q = np.stack([cos * scale, sin * scale], 1) * 8.0 * 1024.0
    k = np.stack([cos / scale, sin / scale], 1) * 1024.0
    tab = np.stack([q, k], 1).astype(np.float32)
    return np.ascontiguousarray(tab.reshape(J, P, 2, 2, DH).transpose(1, 0, 2, 3, 4))


def kernel(**inputs):
    import concourse.bacc as _bacc
    from concourse.bass_utils import run_bass_kernel_spmd as _run

    nc = _bacc.Bacc("TRN2", target_bir_lowering=False, num_devices=1)
    arrays, args = {}, []
    for name, a in laid_out(inputs).items():
        a = np.ascontiguousarray(a)
        arrays[f"in_{name}"] = a
        args.append(nc.dram_tensor(f"in_{name}", a.shape, mybir.dt.from_np(a.dtype), kind="ExternalInput").ap())
    out = nc.dram_tensor("out", (B, T, D), F32, kind="ExternalOutput").ap()
    build(nc, *args, out)
    r = _run(nc, [arrays], core_ids=[0])
    return r.results[0]["out"]
```

```python
from contextlib import ExitStack

import numpy as np

import concourse.bass as bass
from concourse import mybir

F32 = mybir.dt.float32
F32R = mybir.dt.float32r
BF16 = mybir.dt.bfloat16
ALU = mybir.AluOpType
ACT = mybir.ActivationFunctionType
AX = mybir.AxisListType

P = 128
B, T, D = 8, 512, 128
J = T // P
HA, DA = 16, 8
HQ = 4
L = 2
H, DH, W = 8, 64, 64
INNER = H * DH
PAIRS = H // 2
NW = T // W
HID = (D * 4 * 2) // 3
CH = [P, P, HID - 2 * P]
LN_EPS = 1e-5
NORM_MIN2 = 1e-24
SHIFT2 = 2.0 ** 20
MASKED = -3.0e38
EXP_LN = "natural_log_exp_and_others"

A_BANKS = 3
A_UNITS = [(hh, j, q) for hh in range(HQ) for j in range(J) for q in range(HQ)]
A_ORDER = [("xT", 0), ("xT", 1), "qT", "k", "v"] + A_UNITS
A_USE = {s: i for i, s in enumerate(A_ORDER)}
A_PER = len(A_ORDER) // A_BANKS
B_BANKS = 4
AT_UNITS = [(p, g) for p in range(PAIRS) for g in range(2)]
NU = len(AT_UNITS)
PT_LAG, AV_LAG = 2, 3
PR_SLOTS = 3


def b_order():
    out = [("x2T", 0), ("x2T", 1)]
    for l in range(L):
        for i in range(J):
            out += [("q", l, i), ("k", l, i)]
        for i in range(J):
            out += [("qT", l, i), ("kT", l, i)]
        out += [("v", l, i) for i in range(J)]
        for n in range(NU + AV_LAG):
            for name, lag in (("sim", 0), ("pT", PT_LAG), ("av", AV_LAG)):
                if 0 <= n - lag < NU:
                    out.append((name, l, n - lag))
        out += [("wo", l), ("tok", l), ("lnT", l)]
        for c in range(3):
            out += [("gate", l, c), ("up", l, c)]
        out.append(("w2", l))
    return out + [("yT", 0), ("yT", 1)]


UNITS_AFTER = {("enter",): 3}
for _l in range(L):
    UNITS_AFTER["norm", _l] = 4
    UNITS_AFTER.update({("heads", _l, i): 1 for i in range(J)})
    UNITS_AFTER.update({("v", _l, i): 1 for i in range(J)})
    UNITS_AFTER.update({(s, _l, n): 1 for n in range(7 + _l) for s in ("scores", "values")})
    UNITS_AFTER["wo", _l] = 0 if _l else 2
    UNITS_AFTER["ln", _l] = 0 if _l else 3
    UNITS_AFTER["down", _l] = 0 if _l else 2
LEAD = 1
LAG = 3


def units_after(*place):
    names = list(UNITS_AFTER)
    if place not in UNITS_AFTER:
        return range(0)
    first = sum(UNITS_AFTER[n] for n in names[:names.index(place)])
    return range(first, first + UNITS_AFTER[place])


assert sum(UNITS_AFTER.values()) == len(A_UNITS)

B_ORDER = b_order()
B_USE = {s: i for i, s in enumerate(B_ORDER)}
assert len(A_ORDER) % A_BANKS == 0 and len(B_ORDER) % B_BANKS == 0
B_PER = len(B_ORDER) // B_BANKS
GROUPS = [(hh, j) for hh in range(HQ) for j in range(J)]
E_RING = 3
X_SLOTS = 3
N_W = 6
N_COLS = 2 + 3 * L + 6 * L + B
LN_CHAIN = 2 + 3
B_CHAIN = (LN_CHAIN + 3) * L


def build(nc, x, wmod, wqkv1, wqkv, wo, w1, w2, cols_in, rows_in_, rotary, out):
    with ExitStack() as ctx:
        def sb(name, shape, dt=F32):
            return ctx.enter_context(nc.sbuf_tensor(name, shape, dt))

        def sem(name):
            return ctx.enter_context(nc.semaphore(name))

        wqkv1_sb = sb("wqkv1_sb", [D, 3, D])
        wq_sb, wk_sb, wv_sb = (wqkv1_sb[:, n, :] for n in range(3))
        wqkv_sb = sb("wqkv_sb", [D, L, 3 * INNER])
        wo_sb = sb("wo_sb", [P, L, PAIRS, D])
        w1_sb = sb("w1_sb", [D, L, 2 * HID])
        w2_sb = sb("w2_sb", [P, L, 3, D])
        cols = sb("cols", [P, N_COLS])
        bq_col, temp_col = cols[:, 0:1], cols[:, 1:2]
        b2_col, lng_col, lnb_col = ([cols[:, 2 + n * L + l:3 + n * L + l] for l in range(L)] for n in range(3))
        b1_col = [[[cols[0:CH[k], n:n + 1] for k in range(3) for n in [2 + 3 * L + (l * 2 + a) * 3 + k]]
                   for a in range(2)] for l in range(L)]
        c_col = cols[:, N_COLS - B:N_COLS]
        rows = sb("rows", [P, 2 * D + 2 * L * DH])
        bk_bc, bv_bc = rows[:, 0:D], rows[:, D:2 * D]
        scale_bc = rows[:, 2 * D:].rearrange("p (w l d) -> p l w d", w=2, l=L)
        rot = sb("rot", [P, L, J, 2, 2, DH])
        gate_bc = sb("gate_bc", [P, 2, B, D])
        mod_col = sb("mod_col", [D, B, 4])
        cT = sb("cT", [D, 3, B])
        ident = sb("ident", [P, P])
        ident_h = sb("ident_h", [P, P], BF16)
        mask = sb("mask", [P, 8 * 2 * W], BF16)

        x_sb = sb("x_sb", [P, X_SLOTS, J, D])
        stats, mv = sb("stats", [P, J, 6]), sb("mv", [P, J, 2])
        stats1, mv1 = sb("stats1", [P, J, 6]), sb("mv1", [P, J, 2])
        var1, logs1, rstd1, tmp1 = (sb(n, [P, J]) for n in ("var1", "logs1", "rstd1", "tmp1"))
        var_e, logs, rstd0, tmp4 = (sb(n, [P, J]) for n in ("var_e", "logs", "rstd0", "tmp4"))
        qT = sb("qT", [D, J, P])
        hi, lo = sb("hi", [P, 2, J, D], F32R), sb("lo", [P, 2, J, D], F32R)
        k_rows = sb("k_rows", [P, HQ, HQ, T], F32R)
        v_rows = sb("v_rows", [P, HQ, T], F32R)
        neg_max = sb("neg_max", [P, len(A_UNITS)])
        z = sb("z", [P, len(A_UNITS)])
        rz = sb("rz", [P, len(A_UNITS)])
        E = sb("E", [P, E_RING, HQ, T])
        kf = E[:, 0, 0:2, :].rearrange("p n (j f) -> p n j f", j=J)
        hT = E[:, 0, 2, :].rearrange("p (j n) -> p j n", j=J)
        xn = E[:, 0, 3, :].rearrange("p (j f) -> p j f", j=J)
        qz = sb("qz", [P, HQ, J, HQ, 32])

        stats2, mv2 = sb("stats2", [P, J, 6]), sb("mv2", [P, J, 2])
        var2, logs2, rstd02, tmp2 = (sb(n, [P, J]) for n in ("var2", "logs2", "rstd02", "tmp2"))
        y = sb("y", [D, T])
        hs = sb("hs", [D, T])
        rot_work = sb("rot_work", [P, 4, INNER])
        xn2 = rot_work[:, 0].rearrange("p (j f) -> p j f", j=J)
        sq, sinp = rot_work[:, 0:2], rot_work[:, 2:4]
        pr = rot_work[:, 0:PR_SLOTS].rearrange("p s (w n) -> p s w n", w=4)
        work = sb("work", [P, 2 * J * INNER])
        qk = work[:, :].rearrange("p (i w n) -> p i w n", i=J, w=2)
        v_al = work[:, 0:J * INNER].rearrange("p (i n) -> p i n", i=J)
        v_sh = work[:, J * INNER:].rearrange("p (i n) -> p i n", i=J)
        hn = work[:, 0:T].rearrange("p (i n) -> p i n", i=J)
        h2T = work[:, T:2 * T]
        gel = [work[:, (2 + n) * T:(3 + n) * T] for n in range(2)]
        up = [work[:, (4 + n) * T:(5 + n) * T] for n in range(3)]
        ss, rn, nt, nlog = (sb(n, [P, J, 2, H]) for n in ("ss", "rn", "nt", "nlog"))
        kT = sb("kT", [P, PAIRS, W + T])
        q_bd = sb("q_bd", [P, PAIRS, NW, 2, W])
        neg2, z2, rz2 = (sb(n, [P, len(AT_UNITS), 4]) for n in ("neg2", "z2", "rz2"))
        prT = sb("prT", [P, 2, 4, P])
        oT = sb("oT", [P, PAIRS, T])
        gated = prT[:, 0]
        wmod_sb = work[:, 0:6 * D]

        banks = [ctx.enter_context(nc.psum_tensor(f"bank{n}", [P, 512], F32)) for n in range(8)]
        O_BANK = banks[3]
        k_scr = nc.dram_tensor("k_scr", (HQ, HQ, 4, DA, T), F32)
        v_scr = nc.dram_tensor("v_scr", (HQ, HQ, 4, DA, T), F32)

        s_c, s_w, s_rot = sem("s_c"), sem("s_w"), sem("s_rot")
        s_zero, s_ident, s_mask = sem("s_zero"), sem("s_ident"), sem("s_mask")
        s_mask_done, s_mask_both = sem("s_mask_done"), sem("s_mask_both")
        s_silexp, s_sil, s_mod, s_setup = sem("s_silexp"), sem("s_sil"), sem("s_mod"), sem("s_setup")
        s_chain = sem("s_chain")
        x_loaded = sem("x_loaded")
        a_full = [sem(f"a_full{n}") for n in range(A_BANKS)]
        a_free = [sem(f"a_free{n}") for n in range(A_BANKS)]
        a_chain = sem("a_chain")
        ln_chain, split_chain = sem("ln_chain"), sem("split_chain")
        a_var, a_log, a_rstd = sem("a_var"), sem("a_log"), sem("a_rstd")
        xn_ready = sem("xn_ready")
        parts_ready = sem("parts_ready")
        parts_out = sem("parts_out")
        rows_in = sem("rows_in")
        max_ready = sem("max_ready")
        qz_ready = sem("qz_ready")
        av_done = sem("av_done")
        o_read = sem("o_read")
        x2_ready = sem("x2_ready")
        b_full = [sem(f"b_full{n}") for n in range(B_BANKS)]
        b_free = [sem(f"b_free{n}") for n in range(B_BANKS)]
        b_chain, enter_chain = sem("b_chain"), sem("enter_chain")
        x2_var, x2_log, x2_rstd = sem("x2_var"), sem("x2_log"), sem("x2_rstd")
        b_var, b_log, b_rstd = sem("b_var"), sem("b_log"), sem("b_rstd")
        xn2_ready = sem("xn2_ready")
        hs_low, hs_up = sem("hs_low"), sem("hs_up")
        sq_ready = sem("sq_ready")
        rot_sum = sem("rot_sum")
        ss_ready = sem("ss_ready")
        ss_all, ss_log, ss_rsqrt = sem("ss_all"), sem("ss_log"), sem("ss_rsqrt")
        qk_ready = sem("qk_ready")
        q_low = sem("q_low")
        v_pad = sem("v_pad")
        v_shifted = sem("v_shifted")
        max2 = sem("max2")
        rz2_ready = sem("rz2_ready")
        pr_ready = sem("pr_ready")
        out_ready = sem("out_ready")
        stored = sem("stored")

        def a_at(step):
            return A_USE[step] % A_BANKS, A_USE[step] // A_BANKS

        def b_at(step):
            return B_USE[step] % B_BANKS, B_USE[step] // B_BANKS

        credited = a_free + b_free + [rows_in, av_done, parts_out, o_read, stored, ss_ready, rot_sum]

        def passed(eng, s, n):
            eng.wait_ge(s, n + 1)

        def a_take(pe, b, step):
            k, n = a_at(step)
            passed(pe, a_free[k], b * A_PER + n)
            return banks[k], a_full[k]

        def a_see(eng, b, step):
            k, n = a_at(step)
            eng.wait_ge(a_full[k], b * A_PER + n + 1)
            return banks[k], a_free[k]

        def a_done(eng, b, step):
            k, n = a_at(step)
            passed(eng, a_free[k], b * A_PER + n + 1)

        def b_take(pe, b, step, *read):
            k, n = b_at(step)
            need = {k: n}
            for other in read:
                kk, m = b_at(other)
                need[kk] = max(need.get(kk, 0), m + 1)
            for kk, m in need.items():
                passed(pe, b_free[kk], b * B_PER + m)
            return banks[4 + k], b_full[k]

        def b_see(eng, b, step):
            k, n = b_at(step)
            eng.wait_ge(b_full[k], b * B_PER + n + 1)
            return banks[4 + k], b_free[k]

        def b_done(eng, b, *steps):
            need = {}
            for step in steps:
                k, n = b_at(step)
                need[k] = max(need.get(k, 0), n + 1)
            for k, n in need.items():
                passed(eng, b_free[k], b * B_PER + n)

        def stand(eng):
            eng.wait_ge(s_setup, 1)

        def y_done(eng, b, l, half):
            if half:
                b_done(eng, b, ("wo", l))
            elif l:
                b_done(eng, b, ("w2", l - 1))
            else:
                b_done(eng, b, ("x2T", 0), ("x2T", 1))

        block = ctx.enter_context(nc.Block())

        @block.sync
        def _(sp):
            def load(dst, src, s=s_w):
                sp.dma_start(dst, src).then_inc(s, 16)

            load(cols[:], cols_in, s_c)
            load(wmod_sb, wmod, s_c)
            load(wqkv1_sb[:], wqkv1)
            load(rows[:], rows_in_.partition_broadcast(P))
            load(wqkv_sb[:], wqkv)
            load(wo_sb[:], wo)
            load(w1_sb[:], w1)
            load(w2_sb[:], w2)
            for l in range(L):
                load(rot[:, l], rotary, s_rot)
            sp.wait_ge(s_mask_done, 1)
            load(mask[W:P], mask[0:W], s_mask_both)

            def a_load(b):
                sp.dma_start(x_sb[:, b % X_SLOTS], x[b].rearrange("(p j) f -> p j f", j=J)).then_inc(x_loaded, 16)

            def a_parts(b):
                for n, (scr, parts) in enumerate(((k_scr, (hi, hi, lo, lo)), (v_scr, (hi, lo, hi, lo)))):
                    sp.wait_ge(parts_ready, b * 2 + n + 1)
                    for t, part in enumerate(parts):
                        sp.dma_start(scr[:, :, t].rearrange("q h d s -> (q h) d s"),
                                     part[:, n].rearrange("p j f -> p (j f)").bitcast(F32)).then_inc(parts_out, 16)
                passed(sp, parts_out, b * 16 * 8 + 16 * 8)
                for hh in range(HQ):
                    sp.dma_start(k_rows[32 * hh:32 * hh + 32, hh].bitcast(F32),
                                 k_scr[:, hh].rearrange("q t d s -> (t d) q s")).then_inc(rows_in, 16)
                sp.dma_start(v_rows[:].bitcast(F32), v_scr[:].rearrange("q h t d s -> (h t d) q s")).then_inc(rows_in, 16)

            def b_shift_v(b, l):
                b_done(sp, b, ("v", l, J - 1))
                sp.dma_start(v_sh[W:P, :, :], v_al[0:W, :, :]).then_inc(v_shifted, 16)
                sp.dma_start(v_sh[0:W, 1:J, :], v_al[W:P, 0:J - 1, :]).then_inc(v_shifted, 16)

            def b_store(b):
                sp.wait_ge(out_ready, b + 1)
                sp.dma_start(out[b].rearrange("(p j) f -> p j f", j=J), gated).then_inc(stored, 16)

            def batch(b, prep=None):
                if prep is not None:
                    stand(sp)
                    passed(sp, stored, 16 * b)
                    a_load(prep)
                for l in range(L):
                    b_shift_v(b, l)
                if prep is not None:
                    a_parts(prep)
                b_store(b)

            a_load(0)
            sp.wait_ge(x_loaded, 16)
            a_load(1)
            a_parts(0)
            a_parts(1)
            with sp.Fori(0, B - 2) as b:
                batch(b, b + 2)
            batch(B - 2)
            batch(B - 1)
            passed(sp, stored, 16 * B)

        @block.gpsimd
        def _(pool):
            pool.memset(ident[:], 0.0).then_inc(s_zero, 1)
            pool.wait_ge(s_zero, 1)
            pool.affine_select(out=ident[:], in_=ident[:], compare_op=ALU.not_equal, fill=1.0, base=0,
                               pattern=[[-1, P]], channel_multiplier=1).then_inc(s_ident, 1)
            pool.wait_ge(s_ident, 1)
            pool.tensor_copy(ident_h[:], ident[:]).then_inc(s_ident, 1)
            pool.memset(mask[0:W], 0.0).then_inc(s_mask, 1)
            pool.wait_ge(s_mask, 1)
            pool.affine_select(out=mask[0:W], in_=mask[0:W], compare_op=ALU.is_ge, fill=MASKED, base=0,
                               pattern=[[0, 8], [1, 2 * W]], channel_multiplier=-1).then_inc(s_mask, 1)
            pool.wait_ge(s_mask, 2)
            pool.affine_select(out=mask[0:W], in_=mask[0:W], compare_op=ALU.is_ge, fill=MASKED, base=W,
                               pattern=[[0, 8], [-1, 2 * W]], channel_multiplier=1).then_inc(s_mask, 1)
            pool.wait_ge(s_mask, 3)
            pool.memset(mask[0:W, 0:W], MASKED).then_inc(s_mask_done, 1)
            pool.memset(k_rows[:].bitcast(F32), 0.0).then_inc(s_zero, 1)

            def b_rotary(b, l, n):
                i, w = divmod(n, 2)
                b_done(pool, b, ("qk"[w], l, i))
                pool.tensor_tensor(qk[:, i, w, :], qk[:, i, w, :], sinp[:, n % 2, :], ALU.add).then_inc(rot_sum, 1)

            def b_probs(b, l, u):
                pool.wait_ge(rz2_ready, (b * L + l) * NU + u + 1)
                pool.tensor_tensor(pr[:, u % PR_SLOTS], pr[:, u % PR_SLOTS],
                                   rz2[:, u, :].unsqueeze(2).broadcast_to([P, 4, 2 * W]),
                                   ALU.mult).then_inc(pr_ready, 1)

            with pool.Fori(0, B) as b:
                for l in range(L):
                    for n in range(2 * J):
                        b_rotary(b, l, n)
                    for u in range(NU):
                        b_probs(b, l, u)

        @block.scalar
        def _(act):
            act.wait_ge(s_c, 32)
            act.activation(cT[:, 1, :], c_col, ACT.Exp, scale=-1.0).then_inc(s_silexp, 1)
            act.wait_ge(s_setup, 1)
            act.wait_ge(s_w, 16 * N_W)

            def a_rsqrt(b):
                act.wait_ge(a_var, b + 1)
                act.activation(logs[:], var_e[:], ACT.Ln).then_inc(a_log, 1)
                act.wait_ge(a_log, b + 1)
                act.activation(rstd0[:], logs[:], ACT.Exp, scale=-0.5).then_inc(a_rstd, 1)

            def a_modulate(b):
                for n in range(2):
                    stand(act)
                    bank, free = a_see(act, b, ("xT", n))
                    act.activation(hT[:, 2 * n:2 * n + 2], bank[:, 0:2 * P].rearrange("p (j n) -> p j n", j=2),
                                   ACT.Identity, scale=mod_col[:, b, 0:1], bias=mod_col[:, b, 1:2]).then_inc(free, 1)

            def a_queries(b):
                bank, free = a_see(act, b, "qT")
                act.activation(qT[:], bank[:].rearrange("p (j n) -> p j n", j=J), ACT.Identity,
                               bias=bq_col).then_inc(free, 1)

            def a_exp(b, n):
                g, q = divmod(n, HQ)
                bank, free = a_see(act, b, A_UNITS[n])
                act.wait_ge(max_ready, b * len(A_UNITS) + n + 1)
                if q == 0:
                    passed(act, av_done, b * len(GROUPS) + max(g - E_RING + 1, 0))
                act.activation(E[:, g % E_RING, q, :], bank[:], ACT.Exp, bias=neg_max[:, n:n + 1],
                               accum_out=z[:, n:n + 1]).then_inc(free, 1)

            def b_rsqrt(b, l):
                act.wait_ge(b_var, b * L + l + 1)
                act.activation(logs2[:], var2[:], ACT.Ln).then_inc(b_log, 1)
                act.wait_ge(b_log, b * L + l + 1)
                act.activation(rstd02[:], logs2[:], ACT.Exp, scale=-0.5).then_inc(b_rstd, 1)

            def b_enter_rsqrt(b):
                act.wait_ge(x2_var, b + 1)
                act.activation(logs1[:], var1[:], ACT.Ln).then_inc(x2_log, 1)
                act.wait_ge(x2_log, b + 1)
                act.activation(rstd1[:], logs1[:], ACT.Exp, scale=-0.5).then_inc(x2_rstd, 1)

            def b_enter(b):
                y_rows = y[:].rearrange("f (p j) -> f j p", j=J)
                for n in range(2):
                    stand(act)
                    bank, free = b_see(act, b, ("x2T", n))
                    act.activation(y_rows[:, 2 * n:2 * n + 2], bank[:, 0:2 * P].rearrange("p (j n) -> p j n", j=2),
                                   ACT.Identity, scale=mod_col[:, b, 2:3],
                                   bias=mod_col[:, b, 3:4]).then_inc(free, 1)

            def b_shift(b, l, half):
                y_done(act, b, l, half)
                act.activation(hs[0:W, :], y[0:W, :], ACT.Copy).then_inc(hs_low, 1)

            def b_square(b, l, n):
                i, w = divmod(n, 2)
                bank, _ = b_see(act, b, ("qk"[w], l, i))
                passed(act, ss_ready, (b * L + l) * 2 * J + max(n - 1, 0))
                act.activation(sq[:, n % 2], bank[:], ACT.Square).then_inc(sq_ready, 1)

            def b_norm(b, l):
                act.wait_ge(ss_all, b * L + l + 1)
                act.activation(nlog[:], ss[:], ACT.Ln).then_inc(ss_log, 1)
                act.wait_ge(ss_log, b * L + l + 1)
                act.activation(rn[:], nlog[:], ACT.Exp, scale=-0.5).then_inc(ss_rsqrt, 1)

            def b_heads(b, l, i):
                bank, _ = b_see(act, b, ("qT", l, i))
                act.activation(q_bd[0:W, :, 2 * i:2 * i + 2, 0, :],
                               bank[:].rearrange("p (c w t) -> p c w t", c=PAIRS, w=2)[0:W],
                               ACT.Copy).then_inc(q_low, 1)
                bank, free = b_see(act, b, ("kT", l, i))
                act.activation(kT[:, :, W + P * i:W + P * i + P], bank[:].rearrange("p (c t) -> p c t", c=PAIRS),
                               ACT.Copy).then_inc(free, 1)

            def b_values(b, l, i):
                bank, free = b_see(act, b, ("v", l, i))
                act.activation(v_al[:, i, :], bank[:], ACT.Copy).then_inc(free, 1)

            def b_exp(b, l, u):
                bank, free = b_see(act, b, ("sim", l, u))
                act.wait_ge(max2, (b * L + l) * NU + u + 1)
                if u >= PR_SLOTS:
                    b_see(act, b, ("pT", l, u - PR_SLOTS))
                for w in range(4):
                    last = act.activation(pr[:, u % PR_SLOTS, w, :], bank[:, 2 * W * w:2 * W * (w + 1)], ACT.Exp,
                                          bias=neg2[:, u, w:w + 1], accum_out=z2[:, u, w:w + 1])
                last.then_inc(free, 1)

            def b_probsT(b, l, u):
                bank, free = b_see(act, b, ("pT", l, u))
                if l == 0 and u == 0:
                    passed(act, stored, 16 * b)
                if u >= 2:
                    b_see(act, b, ("av", l, u - 2))
                act.activation(prT[:, u % 2], bank[:].rearrange("p (w n) -> p w n", w=4), ACT.Copy).then_inc(free, 1)

            def b_ln(b, l):
                bank, free = b_see(act, b, ("lnT", l))
                act.activation(h2T, bank[:], ACT.Identity, scale=lng_col[l], bias=lnb_col[l]).then_inc(free, 1)

            def b_gelu(b, l, k):
                bank, free = b_see(act, b, ("gate", l, k))
                if k == 2:
                    b_done(act, b, ("up", l, 0))
                act.activation(gel[k % 2][0:CH[k]], bank[0:CH[k]], ACT.Gelu,
                               bias=b1_col[l][1][k]).then_inc(free, 1)

            def a_units(b, *place):
                for n in units_after(*place) if b is not None else ():
                    a_exp(b, n)

            def batch(b, nxt=None, prep=None):
                act.preload_act_table_set(EXP_LN)
                b_enter(b)
                a_units(nxt, "enter")
                for l in range(L):
                    b_shift(b, l, 0)
                    for n in range(2 * J):
                        b_square(b, l, n)
                    a_units(nxt, "norm", l)
                    b_norm(b, l)
                    for i in range(J):
                        b_heads(b, l, i)
                        a_units(nxt, "heads", l, i)
                    for i in range(J):
                        b_values(b, l, i)
                        a_units(nxt, "v", l, i)
                    if l == L - 1 and prep is not None:
                        a_rsqrt(prep)
                    for u in range(NU + PT_LAG):
                        if u < NU:
                            b_exp(b, l, u)
                        a_units(nxt, "scores", l, u)
                        if u >= PT_LAG:
                            b_probsT(b, l, u - PT_LAG)
                        a_units(nxt, "values", l, u)
                    a_units(nxt, "wo", l)
                    b_shift(b, l, 1)
                    if l == L - 1 and prep is not None:
                        a_modulate(prep)
                    if l == L - 1 and nxt is not None:
                        b_enter_rsqrt(nxt)
                    b_rsqrt(b, l)
                    if l == L - 1 and prep is not None:
                        a_queries(prep)
                    a_units(nxt, "ln", l)
                    b_ln(b, l)
                    for k in range(3):
                        b_gelu(b, l, k)
                    if l < L - 1:
                        act.preload_act_table_set(EXP_LN)
                    a_units(nxt, "down", l)

            act.preload_act_table_set(EXP_LN)
            a_rsqrt(0)
            a_modulate(0)
            a_queries(0)
            for n in range(len(A_UNITS)):
                a_exp(0, n)
            a_rsqrt(1)
            a_modulate(1)
            a_queries(1)
            b_enter_rsqrt(0)
            with act.Fori(0, B - 2) as b:
                batch(b, b + 1, b + 2)
            batch(B - 2, B - 1)
            batch(B - 1)

        @block.vector
        def _(dve):
            def chained(s, per):
                state = [0, 0]

                def start(b):
                    state[:] = [b * per, 0]

                def link(ins):
                    state[1] += 1
                    ins.then_inc(s, 1)
                    dve.wait_ge(s, state[0] + state[1])

                def end():
                    assert state[1] == per, state
                return start, link, end

            s_start, s_link, _ = chained(s_chain, 0)
            ln_start, ln_link, ln_end = chained(ln_chain, LN_CHAIN)
            split_start, split_link, split_end = chained(split_chain, 2)
            a_start, a_link, a_end = chained(a_chain, len(GROUPS))
            enter_start, enter_link, enter_end = chained(enter_chain, LN_CHAIN)
            b_start, b_link, b_end = chained(b_chain, B_CHAIN)

            for s in credited:
                dve.sem_inc(s, 1)
            s_start(0)
            s_link(dve.memset(qz[:], 0.0))
            s_link(dve.memset(q_bd[:], 0.0))
            s_link(dve.memset(kT[:, :, 0:W], 0.0))
            s_link(dve.memset(hs[W:P, 0:1], 0.0))
            dve.wait_ge(s_silexp, 1)
            s_link(dve.tensor_scalar(cT[:, 1, :], cT[:, 1, :], 1.0, None, ALU.add))
            s_link(dve.reciprocal(cT[:, 2, :], cT[:, 1, :]))
            dve.tensor_tensor(cT[:, 1, :], c_col, cT[:, 2, :], ALU.mult).then_inc(s_sil, 1)
            dve.wait_ge(s_mod, 1)
            m = banks[0][:, 0:4 * B].rearrange("p (m b) -> p m b", m=4)
            s_link(dve.tensor_scalar(mod_col[:, :, 0], m[:, 0], 1.0, None, ALU.add))
            s_link(dve.tensor_copy(mod_col[:, :, 1], m[:, 1]))
            s_link(dve.tensor_scalar(mod_col[:, :, 2], m[:, 2], 1.0, None, ALU.add))
            s_link(dve.tensor_copy(mod_col[:, :, 3], m[:, 3]))
            for n in range(4):
                s_link(dve.tensor_copy(gate_bc[:, :, 2 * n:2 * n + 2, :],
                                       banks[1 + n][:].rearrange("p (b g f) -> p g b f", b=2, g=2)))
            raw = gate_bc[:].rearrange("p g b f -> p (g b f)")
            sign, size = (E[:, n].rearrange("p q s -> p (q s)") for n in range(2))
            s_link(dve.tensor_scalar(sign, raw, 0.0, 2.0, ALU.is_ge, ALU.mult))
            s_link(dve.scalar_tensor_tensor(size, raw, -1.0, raw, ALU.mult, ALU.max))
            s_link(dve.tensor_scalar(size, size, 0.25, None, ALU.max))
            s_link(dve.scalar_tensor_tensor(raw, sign, -1.0, size, ALU.add, ALU.mult))
            dve.wait_ge(s_rot, 16 * L)
            dve.wait_ge(s_w, 16 * N_W)
            for l in range(L):
                for w in range(2):
                    sc = scale_bc[:, l, w, :]
                    s_link(dve.tensor_tensor(rot[:, l, :, w, 0, :], rot[:, l, :, w, 0, :],
                                             sc.unsqueeze(1).broadcast_to([P, J, DH]), ALU.mult))
                    for a in range(2):
                        r = rot[:, l, :, w, 1, 32 * a:32 * a + 32]
                        s_link(dve.tensor_tensor(r, r, sc[:, 32 - 32 * a:64 - 32 * a].unsqueeze(1)
                                                 .broadcast_to([P, J, 32]), ALU.mult))
            dve.wait_ge(s_zero, 2)
            dve.wait_ge(s_mask_both, 16)
            dve.tensor_scalar(bk_bc, bk_bc, temp_col, None, ALU.mult).then_inc(s_setup, 1)
            dve.wait_ge(s_setup, 1)

            def var_of(src, stats, mv, var, link, ready):
                for j in range(J):
                    last = dve.bn_stats(stats[:, j, :], src[:, j, :])
                link(last)
                dve.tensor_copy(var, ident[:, 0:J])
                for j in range(J):
                    last = dve.bn_aggr(mv[:, j, :], stats[:, j, :])
                link(last)
                dve.tensor_scalar(var, mv[:, :, 1], LN_EPS, None, ALU.add).then_inc(ready, 1)

            def newton(v, r, t, link):
                link(dve.scalar_tensor_tensor(t, v, -0.5, r, ALU.mult, ALU.mult))
                link(dve.tensor_tensor(t, t, r, ALU.mult))
                link(dve.scalar_tensor_tensor(r, t, 1.5, r, ALU.add, ALU.mult))

            def normalize(dst, src, mv, rstd):
                for j in range(J):
                    last = dve.tensor_scalar(dst[:, j, :], src[:, j, :], mv[:, j, 0:1], rstd[:, j:j + 1],
                                             ALU.subtract, ALU.mult)
                return last

            def a_var_of(b):
                ln_start(b)
                stand(dve)
                dve.wait_ge(x_loaded, 16 * b + 16)
                var_of(x_sb[:, b % X_SLOTS], stats, mv, var_e[:], ln_link, a_var)

            def a_normalize(b):
                dve.wait_ge(a_rstd, b + 1)
                newton(var_e[:], rstd0[:], tmp4[:], ln_link)
                normalize(xn, x_sb[:, b % X_SLOTS], mv, rstd0).then_inc(xn_ready, 1)
                ln_end()

            def a_split(b):
                split_start(b)
                for n, step in enumerate("kv"):
                    bank, free = a_see(dve, b, step)
                    src = bank[:].rearrange("p (j f) -> p j f", j=J)
                    if n == 0:
                        passed(dve, parts_out, b * 16 * 8)
                        dve.scalar_tensor_tensor(kf[:, n], src, temp_col,
                                                 bk_bc.unsqueeze(1).broadcast_to([P, J, D]),
                                                 ALU.mult, ALU.add).then_inc(free, 1)
                    else:
                        dve.tensor_tensor(kf[:, n], src, bv_bc.unsqueeze(1).broadcast_to([P, J, D]),
                                          ALU.add).then_inc(free, 1)
                    a_done(dve, b, step)
                    split_link(dve.tensor_copy(hi[:, n], kf[:, n]))
                    dve.tensor_tensor(lo[:, n], kf[:, n], hi[:, n].bitcast(F32), ALU.subtract).then_inc(parts_ready, 1)
                split_end()

            def a_max(b, n):
                bank, _ = a_see(dve, b, A_UNITS[n])
                dve.tensor_reduce(neg_max[:, n:n + 1], bank[:], AX.X, ALU.max, negate=True).then_inc(max_ready, 1)

            def a_weigh(b, g):
                hh, j = GROUPS[g]
                a_done(dve, b, A_UNITS[HQ * g + HQ - 1])
                a_link(dve.reciprocal(rz[:, HQ * g:HQ * g + HQ], z[:, HQ * g:HQ * g + HQ]))
                if g == 0:
                    a_done(dve, b, "qT")
                dve.tensor_tensor(qz[:, hh, j, :, DA * hh:DA * hh + DA],
                                  qT[:, j, :].rearrange("p (q h d) -> p q h d", q=HQ, h=HQ)[:, :, hh, :],
                                  rz[:, HQ * g:HQ * g + HQ].unsqueeze(2).broadcast_to([P, HQ, DA]),
                                  ALU.mult).then_inc(qz_ready, 1)

            def a_residual(b):
                passed(dve, av_done, b * len(GROUPS) + len(GROUPS))
                dve.tensor_tensor(xn, O_BANK[:].rearrange("p (j f) -> p j f", j=J),
                                  gate_bc[:, 0, b, :].unsqueeze(1).broadcast_to([P, J, D]),
                                  ALU.mult).then_inc(o_read, 1)
                passed(dve, o_read, b + 1)
                xb = x_sb[:, b % X_SLOTS]
                dve.tensor_tensor(xb, xb, xn, ALU.add).then_inc(x2_ready, 1)
                a_end()

            def b_enter_var(b):
                enter_start(b)
                stand(dve)
                dve.wait_ge(x2_ready, b + 1)
                var_of(x_sb[:, b % X_SLOTS], stats1, mv1, var1[:], enter_link, x2_var)

            def b_enter_normalize(b):
                dve.wait_ge(x2_rstd, b + 1)
                newton(var1[:], rstd1[:], tmp1[:], enter_link)
                normalize(xn2, x_sb[:, b % X_SLOTS], mv1, rstd1).then_inc(xn2_ready, 1)
                enter_end()

            def b_shift(b, l, half):
                y_done(dve, b, l, half)
                dve.tensor_copy(hs[W:P, 1:T], y[W:P, 0:T - 1]).then_inc(hs_up, 1)

            def b_rotate(b, l, n):
                i, w = divmod(n, 2)
                k = (b * L + l) * 2 * J + n
                dve.wait_ge(sq_ready, k + 1)
                bank, free = b_see(dve, b, ("qk"[w], l, i))
                dve.tensor_tensor(qk[:, i, w, :].rearrange("p (h d) -> p h d", h=H),
                                  bank[:].rearrange("p (h d) -> p h d", h=H),
                                  rot[:, l, i, w, 0, :].unsqueeze(1).broadcast_to([P, H, DH]), ALU.mult)
                passed(dve, rot_sum, (b * L + l) * 2 * J + max(n - 1, 0))
                dve.tensor_tensor(sinp[:, n % 2, :].rearrange("p (h a r) -> p h a r", h=H, a=2),
                                  bank[:].rearrange("p (h a r) -> p h a r", h=H, a=2)[:, :, ::-1, :],
                                  rot[:, l, i, w, 1, :].rearrange("p (a r) -> p a r", a=2).unsqueeze(1)
                                  .broadcast_to([P, H, 2, 32]), ALU.mult).then_inc(free, 1)
                dve.tensor_reduce(ss[:, i, w, :], sq[:, n % 2, :].rearrange("p (h d) -> p h d", h=H),
                                  AX.X, ALU.add).then_inc(ss_ready, 1)

            def b_norm(b, l):
                passed(dve, ss_ready, (b * L + l + 1) * 2 * J)
                dve.tensor_scalar(ss[:], ss[:], NORM_MIN2, SHIFT2, ALU.max, ALU.mult).then_inc(ss_all, 1)
                dve.wait_ge(ss_rsqrt, b * L + l + 1)
                newton(ss[:], rn[:], nt[:], b_link)
                for i in range(J):
                    passed(dve, rot_sum, (b * L + l) * 2 * J + 2 * i + 2)
                    v = qk[:, i].rearrange("p w (h d) -> p (w h) d", h=H)
                    dve.tensor_tensor(v, v, rn[:, i].rearrange("p w h -> p (w h)").unsqueeze(2)
                                      .broadcast_to([P, 2 * H, DH]), ALU.mult).then_inc(qk_ready, 1)

            def b_heads(b, l, i):
                bank, free = b_see(dve, b, ("qT", l, i))
                dve.wait_ge(q_low, (b * L + l) * J + i + 1)
                dve.tensor_copy(q_bd[W:P, :, 2 * i:2 * i + 2, 1, :],
                                bank[:].rearrange("p (c w t) -> p c w t", c=PAIRS, w=2)[W:P]).then_inc(free, 1)

            def b_pad_v(b, l):
                b_see(dve, b, ("v", l, 0))
                dve.memset(v_sh[0:W, 0, :], 0.0).then_inc(v_pad, 1)

            def b_max(b, l, u):
                bank, _ = b_see(dve, b, ("sim", l, u))
                dve.tensor_reduce(neg2[:, u, :], bank[:].rearrange("p (w n) -> p w n", w=4), AX.X, ALU.max,
                                  negate=True).then_inc(max2, 1)

            def b_sums(b, l, u):
                b_done(dve, b, ("sim", l, u))
                dve.reciprocal(rz2[:, u, :], z2[:, u, :]).then_inc(rz2_ready, 1)

            def b_heads_out(b, l, u):
                p, g = AT_UNITS[u]
                bank, free = b_see(dve, b, ("av", l, u))
                src = bank[:].rearrange("p (w h t) -> p w h t", w=4, h=2)
                dst = oT[:, p, 4 * W * g:4 * W * (g + 1)].rearrange("p (w t) -> p w t", w=4)
                dve.tensor_copy(dst[0:W], src[0:W, :, 0, :])
                dve.tensor_copy(dst[W:P], src[W:P, :, 1, :]).then_inc(free, 1)

            def b_residual(b, l):
                bank, free = b_see(dve, b, ("wo", l))
                y_read(dve, b, l, 0)
                dve.tensor_tensor(y[:], bank[:], y[:], ALU.add).then_inc(free, 1)

            def y_read(dve, b, l, half):
                dve.wait_ge(hs_low, (b * L + l) * 2 + half + 1)
                dve.wait_ge(hs_up, (b * L + l) * 2 + half + 1)

            def b_ln_var(b, l):
                stand(dve)
                bank, _ = b_see(dve, b, ("tok", l))
                var_of(bank[:].rearrange("p (j f) -> p j f", j=J), stats2, mv2, var2[:], b_link, b_var)

            def b_ln(b, l):
                bank, free = b_see(dve, b, ("tok", l))
                src = bank[:].rearrange("p (j f) -> p j f", j=J)
                dve.wait_ge(b_rstd, b * L + l + 1)
                newton(var2[:], rstd02[:], tmp2[:], b_link)
                normalize(hn, src, mv2, rstd02).then_inc(free, 1)

            def b_up(b, l, k):
                bank, free = b_see(dve, b, ("up", l, k))
                b_done(dve, b, ("gate", l, k))
                dve.scalar_tensor_tensor(up[k][0:CH[k]], bank[0:CH[k]], b1_col[l][0][k],
                                         gel[k % 2][0:CH[k]], ALU.add, ALU.mult).then_inc(free, 1)

            def b_down(b, l):
                bank, free = b_see(dve, b, ("w2", l))
                y_read(dve, b, l, 1)
                dve.scalar_tensor_tensor(y[:], bank[:], b2_col[l], y[:], ALU.add, ALU.add).then_inc(free, 1)

            def b_out(b):
                for n in range(2):
                    bank, free = b_see(dve, b, ("yT", n))
                    dve.tensor_tensor(gated[:, 2 * n:2 * n + 2], bank[:, 0:2 * P].rearrange("p (j f) -> p j f", j=2),
                                      gate_bc[:, 1, b, :].unsqueeze(1).broadcast_to([P, 2, D]),
                                      ALU.mult).then_inc(free, 1)
                b_done(dve, b, ("yT", 0), ("yT", 1))
                dve.tensor_tensor(gated, gated, x_sb[:, b % X_SLOTS], ALU.add).then_inc(out_ready, 1)
                b_end()

            def a_unit(b, n):
                if n == 0:
                    a_start(b)
                if n < len(A_UNITS):
                    a_max(b, n)
                if n >= HQ - 1 + LAG - 1 and (n - (HQ - 1 + LAG - 1)) % HQ == 0:
                    a_weigh(b, (n - (HQ - 1 + LAG - 1)) // HQ)

            def a_units(b, *place):
                for n in units_after(*place) if b is not None else ():
                    a_unit(b, n)

            def a_finish(b):
                for n in range(len(A_UNITS), len(A_UNITS) + LAG):
                    a_unit(b, n)

            def batch(b, nxt=None, prep=None):
                a_units(nxt, "enter")
                b_start(b)
                for l in range(L):
                    b_shift(b, l, 0)
                    for n in range(2 * J):
                        b_rotate(b, l, n)
                    a_units(nxt, "norm", l)
                    b_norm(b, l)
                    for i in range(J):
                        b_heads(b, l, i)
                        a_units(nxt, "heads", l, i)
                    b_pad_v(b, l)
                    for i in range(J):
                        a_units(nxt, "v", l, i)
                    if l == L - 1 and prep is not None:
                        a_var_of(prep)
                    for u in range(NU + AV_LAG):
                        if u < NU:
                            b_max(b, l, u)
                        a_units(nxt, "scores", l, u)
                        if 1 <= u <= NU:
                            b_sums(b, l, u - 1)
                        if u >= AV_LAG:
                            b_heads_out(b, l, u - AV_LAG)
                        a_units(nxt, "values", l, u)
                        if l == L - 1 and u == NU and nxt is not None:
                            a_finish(nxt)
                    if l == L - 1 and nxt is not None:
                        a_residual(nxt)
                        if prep is not None:
                            a_normalize(prep)
                    a_units(nxt, "wo", l)
                    b_residual(b, l)
                    b_shift(b, l, 1)
                    if l == L - 1 and nxt is not None:
                        b_enter_var(nxt)
                    b_ln_var(b, l)
                    if l == L - 1 and nxt is not None:
                        b_enter_normalize(nxt)
                    a_units(nxt, "ln", l)
                    b_ln(b, l)
                    if l == L - 1 and prep is not None:
                        a_split(prep)
                    for k in range(3):
                        b_up(b, l, k)
                    a_units(nxt, "down", l)
                    b_down(b, l)
                b_out(b)

            a_var_of(0)
            a_normalize(0)
            a_split(0)
            for n in range(len(A_UNITS)):
                a_unit(0, n)
            a_var_of(1)
            a_finish(0)
            a_residual(0)
            a_normalize(1)
            b_enter_var(0)
            a_split(1)
            b_enter_normalize(0)
            with dve.Fori(0, B - 2) as b:
                batch(b, b + 1, b + 2)
            batch(B - 2, B - 1)
            batch(B - 1)

        @block.tensor
        def _(pe):
            pe.wait_ge(s_c, 32)
            pe.wait_ge(s_sil, 1)
            sil = cT[:, 1, :]
            for n, m in enumerate((1, 0, 4, 3)):
                pe.matmul(banks[0][:, B * n:B * (n + 1)], wmod_sb[:, D * m:D * (m + 1)], sil, start=True, stop=True)
            for b in range(B):
                for n, m in enumerate((2, 5)):
                    o = (b % 2) * 2 * D + n * D
                    last = pe.matmul(banks[1 + b // 2][:, o:o + D], sil[:, b:b + 1].broadcast_to([D, P]),
                                     wmod_sb[:, D * m:D * (m + 1)], start=True, stop=True)
            last.then_inc(s_mod, 1)
            pe.wait_ge(s_setup, 1)
            pe.wait_ge(s_w, 16 * N_W)
            pe.wait_ge(s_ident, 2)

            def a_transpose(b):
                pe.wait_ge(xn_ready, b + 1)
                for n in range(2):
                    bank, full = a_take(pe, b, ("xT", n))
                    for j in range(2):
                        last = pe.transpose(bank[:, P * j:P * (j + 1)], xn[:, 2 * n + j, :], ident[:])
                    last.then_inc(full, 1)

            def a_project(b):
                for n in range(2):
                    a_done(pe, b, ("xT", n))
                bank, full = a_take(pe, b, "qT")
                pe.matmul(bank[:], wq_sb, E[:, 0, 2, :], start=True, stop=True).then_inc(full, 1)
                for step, w in (("k", wk_sb), ("v", wv_sb)):
                    bank, full = a_take(pe, b, step)
                    for j in range(J):
                        last = pe.matmul(bank[:, D * j:D * (j + 1)], hT[:, j, :], w, start=True, stop=True)
                    last.then_inc(full, 1)

            def a_scores(b, n):
                hh, j, q = A_UNITS[n]
                if n == 0:
                    passed(pe, rows_in, (b + 1) * 16 * (HQ + 1))
                bank, full = a_take(pe, b, A_UNITS[n])
                pe.matmul(bank[:], k_rows[:, hh, q, P * j:P * (j + 1)], v_rows[:, q, :],
                          start=True, stop=True).then_inc(full, 1)

            def a_values(b, g):
                hh, j = GROUPS[g]
                pe.wait_ge(qz_ready, b * len(GROUPS) + g + 1)
                if g == 0:
                    passed(pe, o_read, b)
                for q in range(HQ):
                    last = pe.matmul(O_BANK[32 * q:32 * q + 32, :], qz[:, hh, j, q, :], E[:, g % E_RING, q, :],
                                     start=(g == 0), stop=(g == len(GROUPS) - 1))
                last.then_inc(av_done, 1)

            def b_enter(b):
                pe.wait_ge(xn2_ready, b + 1)
                for n in range(2):
                    bank, full = b_take(pe, b, ("x2T", n))
                    for j in range(2):
                        last = pe.transpose(bank[:, P * j:P * (j + 1)], xn2[:, 2 * n + j, :], ident[:])
                    last.then_inc(full, 1)

            def hs_wait(b, l, half):
                pe.wait_ge(hs_low, (b * L + l) * 2 + half + 1)
                pe.wait_ge(hs_up, (b * L + l) * 2 + half + 1)

            def b_project(b, l, i, w):
                bank, full = b_take(pe, b, ("qkv"[w], l, i))
                pe.matmul(bank[:], hs[:, P * i:P * (i + 1)], wqkv_sb[:, l, INNER * w:INNER * (w + 1)],
                          start=True, stop=True).then_inc(full, 1)

            def b_heads(b, l, i):
                pe.wait_ge(qk_ready, (b * L + l) * J + i + 1)
                for w in range(2):
                    bank, full = b_take(pe, b, (("qT", "kT")[w], l, i))
                    for p in range(PAIRS):
                        last = pe.transpose(bank[:, P * p:P * (p + 1)], qk[:, i, w, P * p:P * (p + 1)], ident[:])
                    last.then_inc(full, 1)

            def b_scores(b, l, u):
                p, g = AT_UNITS[u]
                tiles = [(s, l, 2 * g + i) for s in ("qT", "kT") for i in range(2)] if u < 2 else []
                bank, full = b_take(pe, b, ("sim", l, u), *tiles)
                pe.matmul(bank[:], ident_h[:], mask[:, (1 if g else 0) * 512:(2 if g else 1) * 512],
                          start=True, stop=False)
                for w in range(4):
                    n = 4 * g + w
                    last = pe.matmul(bank[:, 2 * W * w:2 * W * (w + 1)], q_bd[:, p, n].rearrange("p h t -> p (h t)"),
                                     kT[:, p, W * n:W * n + 2 * W], start=False, stop=(w == 3))
                last.then_inc(full, 1)

            def b_probsT(b, l, u):
                pe.wait_ge(pr_ready, (b * L + l) * NU + u + 1)
                bank, full = b_take(pe, b, ("pT", l, u))
                for w in range(4):
                    last = pe.transpose(bank[:, P * w:P * (w + 1)], pr[:, u % PR_SLOTS, w, :], ident[:])
                last.then_inc(full, 1)

            def b_values(b, l, u):
                p, g = AT_UNITS[u]
                if u == 0:
                    pe.wait_ge(v_shifted, (b * L + l + 1) * 32)
                    pe.wait_ge(v_pad, b * L + l + 1)
                tiles = [("v", l, i) for i in range(J)] if u == 0 else []
                bank, full = b_take(pe, b, ("av", l, u), ("pT", l, u), *tiles)
                for w in range(4):
                    n = 4 * g + w
                    v = v_al[:, n // 2] if n % 2 else v_sh[:, n // 2]
                    last = pe.matmul(bank[:, P * w:P * (w + 1)], v[:, P * p:P * (p + 1)], prT[:, u % 2, w, :],
                                     start=True, stop=True)
                last.then_inc(full, 1)

            def b_project_out(b, l):
                bank, full = b_take(pe, b, ("wo", l), *(("av", l, u) for u in range(NU)))
                for p in range(PAIRS):
                    last = pe.matmul(bank[:], wo_sb[:, l, p, :], oT[:, p, :], start=(p == 0), stop=(p == PAIRS - 1))
                last.then_inc(full, 1)

            def b_ln_in(b, l):
                hs_wait(b, l, 1)
                bank, full = b_take(pe, b, ("tok", l))
                for i in range(J):
                    last = pe.transpose(bank[:, P * i:P * (i + 1)], hs[:, P * i:P * (i + 1)], ident[:])
                last.then_inc(full, 1)

            def b_ln_out(b, l):
                bank, full = b_take(pe, b, ("lnT", l), ("tok", l))
                for i in range(J):
                    last = pe.transpose(bank[:, P * i:P * (i + 1)], hn[:, i, :], ident[:])
                last.then_inc(full, 1)

            def b_hidden(b, l, k, a):
                bank, full = b_take(pe, b, (("up", "gate")[a], l, k), ("lnT", l))
                o = a * HID + P * k
                pe.matmul(bank[0:CH[k]], w1_sb[:, l, o:o + CH[k]], h2T, start=True, stop=True).then_inc(full, 1)

            def b_down(b, l):
                bank, full = b_take(pe, b, ("w2", l), *(("up", l, k) for k in range(3)))
                for k in range(3):
                    last = pe.matmul(bank[:], w2_sb[0:CH[k], l, k, :], up[k][0:CH[k]], start=(k == 0), stop=(k == 2))
                last.then_inc(full, 1)

            def b_leave(b):
                y_rows = y[:].rearrange("f (p j) -> f j p", j=J)
                for n in range(2):
                    bank, full = b_take(pe, b, ("yT", n), ("w2", L - 1))
                    for j in range(2):
                        last = pe.transpose(bank[:, P * j:P * (j + 1)], y_rows[:, 2 * n + j, :], ident[:])
                    last.then_inc(full, 1)

            def a_unit(b, n):
                if n + LEAD < len(A_UNITS):
                    a_scores(b, n + LEAD)
                if n >= HQ - 1 + LAG and (n - (HQ - 1 + LAG)) % HQ == 0:
                    a_values(b, (n - (HQ - 1 + LAG)) // HQ)

            def a_units(b, *place):
                for n in units_after(*place) if b is not None else ():
                    if n == 0:
                        a_begin(b)
                    a_unit(b, n)

            def a_begin(b):
                for n in range(LEAD):
                    a_scores(b, n)

            def a_finish(b):
                for n in range(len(A_UNITS), len(A_UNITS) + LAG):
                    a_unit(b, n)

            def batch(b, nxt=None, prep=None):
                b_enter(b)
                a_units(nxt, "enter")
                for l in range(L):
                    hs_wait(b, l, 0)
                    for i in range(J):
                        for w in range(2):
                            b_project(b, l, i, w)
                    a_units(nxt, "norm", l)
                    for i in range(J):
                        b_heads(b, l, i)
                        a_units(nxt, "heads", l, i)
                    for i in range(J):
                        b_project(b, l, i, 2)
                        a_units(nxt, "v", l, i)
                    for u in range(NU + AV_LAG):
                        if u < NU:
                            b_scores(b, l, u)
                        a_units(nxt, "scores", l, u)
                        if PT_LAG <= u < NU + PT_LAG:
                            b_probsT(b, l, u - PT_LAG)
                        if u >= AV_LAG:
                            b_values(b, l, u - AV_LAG)
                        a_units(nxt, "values", l, u)
                        if l == L - 1 and u == NU and nxt is not None:
                            a_finish(nxt)
                    b_project_out(b, l)
                    a_units(nxt, "wo", l)
                    if l == L - 1 and prep is not None:
                        a_transpose(prep)
                    b_ln_in(b, l)
                    if l == L - 1 and prep is not None:
                        a_project(prep)
                    a_units(nxt, "ln", l)
                    b_ln_out(b, l)
                    for k in range(3):
                        b_hidden(b, l, k, 1)
                        b_hidden(b, l, k, 0)
                    a_units(nxt, "down", l)
                    b_down(b, l)
                b_leave(b)

            a_transpose(0)
            a_project(0)
            a_begin(0)
            for n in range(len(A_UNITS)):
                a_unit(0, n)
            a_finish(0)
            a_transpose(1)
            a_project(1)
            with pe.Fori(0, B - 2) as b:
                batch(b, b + 1, b + 2)
            batch(B - 2, B - 1)
            batch(B - 1)


def laid_out(inputs):
    a = {n[3:]: np.asarray(v) for n, v in inputs.items()}
    cols = np.zeros((P, N_COLS), np.float32)
    cols[:, 0] = a["attn_bq"]
    cols[:, 1] = np.repeat(a["attn_temperature"].reshape(-1), DA)
    for l in range(L):
        cols[:, 2 + l] = a["ffn_b2"][l]
        cols[:, 2 + L + l] = a["ffn_ln_g"][l]
        cols[:, 2 + 2 * L + l] = a["ffn_ln_b"][l]
        for h in range(2):
            for k in range(3):
                cols[:CH[k], 2 + 3 * L + (l * 2 + h) * 3 + k] = a["ffn_b1"][l, h * HID + P * k:][:CH[k]]
    cols[:, N_COLS - B:] = a["c"].T
    w2 = np.zeros((L, 3 * P, D), np.float32)
    w2[:, :HID] = a["ffn_w2"]
    return {
        "x": a["attn_x"], "wmod": a["wmod"],
        "wqkv1": np.stack([a["attn_Wq"], a["attn_Wk"], a["attn_Wv"]], 1),
        "wqkv": a["ffn_wqkv"].transpose(1, 0, 2),
        "wo": a["ffn_wo"].reshape(L, PAIRS, P, D).transpose(2, 0, 1, 3),
        "w1": a["ffn_w1"].transpose(1, 0, 2),
        "w2": w2.reshape(L, 3, P, D).transpose(2, 0, 1, 3),
        "cols": cols,
        "rows": np.concatenate([a["attn_bk"], a["attn_bv"], a["ffn_q_scale"].reshape(-1), a["ffn_k_scale"].reshape(-1)]),
        "rotary": rotary_tables(),
    }


def rotary_tables():
    half = np.arange(0, DH, 2, dtype=np.float32)
    inv = (np.float32(1.0) / np.float32(10000.0) ** (half / np.float32(DH))).astype(np.float32)
    t = np.arange(T, dtype=np.float32)
    freqs = t[:, None] * inv[None, :]
    freqs = np.concatenate([freqs, freqs], -1).astype(np.float64)
    base = (half + np.float32(0.4 * DH)) / np.float32(1.4 * DH)
    power = (t - T // 2) / np.float32(W // 2)
    scale = base[None, :].astype(np.float32) ** power[:, None]
    scale = np.concatenate([scale, scale], -1).astype(np.float64)
    sign = np.where(np.arange(DH) < DH // 2, -1.0, 1.0)
    cos, sin = np.cos(freqs), np.sin(freqs) * sign
    q = np.stack([cos * scale, sin * scale], 1) * 8.0 * 1024.0
    k = np.stack([cos / scale, sin / scale], 1) * 1024.0
    tab = np.stack([q, k], 1).astype(np.float32)
    return np.ascontiguousarray(tab.reshape(J, P, 2, 2, DH).transpose(1, 0, 2, 3, 4))


def kernel(**inputs):
    import concourse.bacc as _bacc
    from concourse.bass_utils import run_bass_kernel_spmd as _run

    nc = _bacc.Bacc("TRN2", target_bir_lowering=False, num_devices=1)
    arrays, args = {}, []
    for name, a in laid_out(inputs).items():
        a = np.ascontiguousarray(a)
        arrays[f"in_{name}"] = a
        args.append(nc.dram_tensor(f"in_{name}", a.shape, mybir.dt.from_np(a.dtype), kind="ExternalInput").ap())
    out = nc.dram_tensor("out", (B, T, D), F32, kind="ExternalOutput").ap()
    build(nc, *args, out)
    r = _run(nc, [arrays], core_ids=[0])
    return r.results[0]["out"]
```

```python
from contextlib import ExitStack

import numpy as np

import concourse.bass as bass
from concourse import mybir

F32 = mybir.dt.float32
F32R = mybir.dt.float32r
BF16 = mybir.dt.bfloat16
ALU = mybir.AluOpType
ACT = mybir.ActivationFunctionType
AX = mybir.AxisListType

P = 128
B, T, D = 8, 512, 128
J = T // P
HA, DA = 16, 8
HQ = 4
L = 2
H, DH, W = 8, 64, 64
INNER = H * DH
PAIRS = H // 2
NW = T // W
HID = (D * 4 * 2) // 3
CH = [P, P, HID - 2 * P]
LN_EPS = 1e-5
NORM_MIN2 = 1e-24
SHIFT2 = 2.0 ** 20
MASKED = -3.0e38
EXP_LN = "natural_log_exp_and_others"

A_BANKS = 3
A_UNITS = [(hh, j, q) for hh in range(HQ) for j in range(J) for q in range(HQ)]
A_ORDER = ["xT", "qT", "k", "v"] + A_UNITS + ["x2T"]
A_USE = {s: i for i, s in enumerate(A_ORDER)}
A_PER = len(A_ORDER) // A_BANKS
B_BANKS = 4
AT_UNITS = [(p, g) for p in range(PAIRS) for g in range(2)]
NU = len(AT_UNITS)
PT_LAG, AV_LAG = 2, 3
PR_SLOTS = 3


def b_order():
    out = []
    for l in range(L):
        for i in range(J):
            out += [("q", l, i), ("k", l, i), ("v", l, i)]
        for i in range(J):
            out += [("qT", l, i), ("kT", l, i)]
        for n in range(NU + AV_LAG):
            for name, lag in (("sim", 0), ("pT", PT_LAG), ("av", AV_LAG)):
                if 0 <= n - lag < NU:
                    out.append((name, l, n - lag))
        out += [("wo", l), ("tok", l), ("lnT", l)]
        out += [(name, l, c) for name in ("gate", "up") for c in range(3)] + [("w2", l)]
    return out + [("yT", j) for j in range(J)]


NORM, ATT = (4, 4), (7, 8)
UNITS_AFTER = {}
for _l in range(L):
    UNITS_AFTER["shift", _l] = 2 * _l
    UNITS_AFTER["norm", _l] = NORM[_l]
    UNITS_AFTER.update({("heads", _l, i): 2 for i in range(J)})
    UNITS_AFTER.update({(s, _l, n): 1 for n in range(ATT[_l]) for s in ("scores", "values")})
    if _l == 0:
        UNITS_AFTER.update({("wo", _l): 2, ("ln", _l): 3, ("up", _l): 3})
LEAD = 1
LAG = 3


def units_after(*place):
    names = list(UNITS_AFTER)
    if place not in UNITS_AFTER:
        return range(0)
    first = sum(UNITS_AFTER[n] for n in names[:names.index(place)])
    return range(first, first + UNITS_AFTER[place])


assert sum(UNITS_AFTER.values()) == len(A_UNITS)

B_ORDER = b_order()
B_USE = {s: i for i, s in enumerate(B_ORDER)}
assert len(A_ORDER) % A_BANKS == 0 and len(B_ORDER) % B_BANKS == 0
B_PER = len(B_ORDER) // B_BANKS
GROUPS = [(hh, j) for hh in range(HQ) for j in range(J)]
E_RING = 3
X_SLOTS = 3
N_W = 4
QZ_SLOTS = 2
N_COLS = 2 + 3 * L + 6 * L + B
LN_CHAIN = 2 + 3
B_CHAIN = (LN_CHAIN + 3) * L


def build(nc, x, wmod, wqkv1, wqkv, wo, w1, w2, cols_in, rows_in_, rotary, out):
    with ExitStack() as ctx:
        def sb(name, shape, dt=F32):
            return ctx.enter_context(nc.sbuf_tensor(name, shape, dt))

        def sem(name):
            return ctx.enter_context(nc.semaphore(name))

        wqkv1_sb = sb("wqkv1_sb", [D, 3, D])
        wq_sb, wk_sb, wv_sb = (wqkv1_sb[:, n, :] for n in range(3))
        wqkv_sb = sb("wqkv_sb", [D, L, 3 * INNER])
        wo_sb = sb("wo_sb", [P, L, PAIRS, D])
        w1_sb = sb("w1_sb", [D, L, 2 * HID])
        w2_sb = sb("w2_sb", [P, L, 3, D])
        cols = sb("cols", [P, N_COLS])
        bq_col, temp_col = cols[:, 0:1], cols[:, 1:2]
        b2_col, lng_col, lnb_col = ([cols[:, 2 + n * L + l:3 + n * L + l] for l in range(L)] for n in range(3))
        b1_col = [[[cols[0:CH[k], n:n + 1] for k in range(3) for n in [2 + 3 * L + (l * 2 + a) * 3 + k]]
                   for a in range(2)] for l in range(L)]
        c_col = cols[:, N_COLS - B:N_COLS]
        rows = sb("rows", [P, 2 * D + 2 * L * DH])
        bk_bc, bv_bc = rows[:, 0:D], rows[:, D:2 * D]
        scale_bc = rows[:, 2 * D:].rearrange("p (w l d) -> p l w d", w=2, l=L)
        rot = sb("rot", [P, L, J, 2, 2, DH])
        gate_bc = sb("gate_bc", [P, 2, B, D])
        mod_col = sb("mod_col", [D, B, 4])
        cT = sb("cT", [D, 2, B])
        ident = sb("ident", [P, P])
        ident_h = sb("ident_h", [P, P], BF16)
        mask = sb("mask", [P, 5 * 2 * W], BF16)

        x_sb = sb("x_sb", [P, X_SLOTS, J, D])
        stats, mv = sb("stats", [P, J, 6]), sb("mv", [P, J, 2])
        stats1, mv1 = sb("stats1", [P, J, 6]), sb("mv1", [P, J, 2])
        var1, logs1, rstd1, tmp1 = (sb(n, [P, J]) for n in ("var1", "logs1", "rstd1", "tmp1"))
        var_e, logs, rstd0, tmp4 = (sb(n, [P, J]) for n in ("var_e", "logs", "rstd0", "tmp4"))
        qT = sb("qT", [D, J, P])
        hi, lo = sb("hi", [P, 2, J, D], F32R), sb("lo", [P, 2, J, D], F32R)
        k_rows = sb("k_rows", [P, HQ, HQ, T], F32R)
        v_rows = sb("v_rows", [P, HQ, T], F32R)
        neg_max = sb("neg_max", [P, len(A_UNITS)])
        z = sb("z", [P, len(A_UNITS)])
        rz = sb("rz", [P, 2 * HQ])
        E = sb("E", [P, E_RING, HQ, T])
        kf = E[:, 0, 0:2, :].rearrange("p n (j f) -> p n j f", j=J)
        hT = E[:, 0, 2, :].rearrange("p (j n) -> p j n", j=J)
        xn = E[:, 0, 3, :].rearrange("p (j f) -> p j f", j=J)
        qz = sb("qz", [P, HQ, QZ_SLOTS, HQ, 32])

        stats2, mv2 = sb("stats2", [P, J, 6]), sb("mv2", [P, J, 2])
        var2, logs2, rstd02, tmp2 = (sb(n, [P, J]) for n in ("var2", "logs2", "rstd02", "tmp2"))
        y = sb("y", [D, T])
        y_in = sb("y_in", [D, T])
        hs = sb("hs", [D, T])
        rot_work = sb("rot_work", [P, 4, INNER])
        xn2 = rot_work[:, 0].rearrange("p (j f) -> p j f", j=J)
        sq, sinp = rot_work[:, 0:2], rot_work[:, 2:4]
        pr = rot_work[:, 0:PR_SLOTS].rearrange("p s (w n) -> p s w n", w=4)
        work = sb("work", [P, 2 * J * INNER])
        qk = work[:, :].rearrange("p (i w n) -> p i w n", i=J, w=2)
        v_al = sb("v_al", [P, J, INNER])
        v_sh = work[:, J * INNER:].rearrange("p (i n) -> p i n", i=J)
        hn = work[:, 0:T].rearrange("p (i n) -> p i n", i=J)
        h2T = work[:, T:2 * T]
        gel = [work[:, n * T:(n + 1) * T] for n in (2, 3, 0)]
        up = [work[:, (4 + n) * T:(5 + n) * T] for n in range(3)]
        ss, rn, nt, nlog = (sb(n, [P, J, 2, H]) for n in ("ss", "rn", "nt", "nlog"))
        kT = sb("kT", [P, PAIRS, W + T])
        q_bd = sb("q_bd", [P, PAIRS, NW, 2, W])
        neg2, z2, rz2 = (sb(n, [P, len(AT_UNITS), 4]) for n in ("neg2", "z2", "rz2"))
        prT = sb("prT", [P, 2, 4, P])
        oT = sb("oT", [P, PAIRS, T])
        gated = prT[:, 0]
        wmod_sb = work[:, 0:6 * D]

        banks = [ctx.enter_context(nc.psum_tensor(f"bank{n}", [P, 512], F32)) for n in range(8)]
        O_BANK = banks[3]
        k_scr = nc.dram_tensor("k_scr", (HQ, HQ, 4, DA, T), F32)
        v_scr = nc.dram_tensor("v_scr", (HQ, HQ, 4, DA, T), F32)

        s_c, s_first, s_w, s_rot = sem("s_c"), sem("s_first"), sem("s_w"), sem("s_rot")
        s_zero, s_ident, s_mask = sem("s_zero"), sem("s_ident"), sem("s_mask")
        s_mask_done, s_mask_both = sem("s_mask_done"), sem("s_mask_both")
        s_silexp, s_sil, s_mod, s_setup = sem("s_silexp"), sem("s_sil"), sem("s_mod"), sem("s_setup")
        s_gates = sem("s_gates")
        s_chain = sem("s_chain")
        x_loaded = sem("x_loaded")
        a_full = [sem(f"a_full{n}") for n in range(A_BANKS)]
        a_free = [sem(f"a_free{n}") for n in range(A_BANKS)]
        a_chain = sem("a_chain")
        ln_chain, split_chain = sem("ln_chain"), sem("split_chain")
        a_var, a_log, a_rstd = sem("a_var"), sem("a_log"), sem("a_rstd")
        xn_ready = sem("xn_ready")
        parts_ready = sem("parts_ready")
        parts_out = sem("parts_out")
        rows_in = sem("rows_in")
        max_ready = sem("max_ready")
        qz_ready = sem("qz_ready")
        av_done = sem("av_done")
        o_read = sem("o_read")
        x2_ready = sem("x2_ready")
        b_full = [sem(f"b_full{n}") for n in range(B_BANKS)]
        b_free = [sem(f"b_free{n}") for n in range(B_BANKS)]
        b_chain, enter_chain = sem("b_chain"), sem("enter_chain")
        x2_var, x2_log, x2_rstd = sem("x2_var"), sem("x2_log"), sem("x2_rstd")
        b_var, b_log, b_rstd = sem("b_var"), sem("b_log"), sem("b_rstd")
        xn2_ready = sem("xn2_ready")
        hs_low, hs_up = sem("hs_low"), sem("hs_up")
        sq_ready = sem("sq_ready")
        k_copied, k_cos = sem("k_copied"), sem("k_cos")
        rot_sum = sem("rot_sum")
        ss_ready = sem("ss_ready")
        ss_all, ss_log, ss_rsqrt = sem("ss_all"), sem("ss_log"), sem("ss_rsqrt")
        q_ready, k_ready = sem("q_ready"), sem("k_ready")
        q_low = sem("q_low")
        v_pad = sem("v_pad")
        v_shifted = sem("v_shifted")
        max2 = sem("max2")
        rz2_ready = sem("rz2_ready")
        pr_ready = sem("pr_ready")
        out_ready = sem("out_ready")
        stored = sem("stored")

        def a_at(step):
            return A_USE[step] % A_BANKS, A_USE[step] // A_BANKS

        def b_at(step):
            return B_USE[step] % B_BANKS, B_USE[step] // B_BANKS

        credited = a_free + b_free + [rows_in, av_done, parts_out, o_read, stored, ss_ready, rot_sum]

        def passed(eng, s, n):
            eng.wait_ge(s, n + 1)

        def a_take(pe, b, step):
            k, n = a_at(step)
            passed(pe, a_free[k], b * A_PER + n)
            return banks[k], a_full[k]

        def a_see(eng, b, step):
            k, n = a_at(step)
            eng.wait_ge(a_full[k], b * A_PER + n + 1)
            return banks[k], a_free[k]

        def a_done(eng, b, step):
            k, n = a_at(step)
            passed(eng, a_free[k], b * A_PER + n + 1)

        def b_take(pe, b, step, *read):
            k, n = b_at(step)
            need = {k: n}
            for other in read:
                kk, m = b_at(other)
                need[kk] = max(need.get(kk, 0), m + 1)
            for kk, m in need.items():
                passed(pe, b_free[kk], b * B_PER + m)
            return banks[4 + k], b_full[k]

        def b_see(eng, b, step):
            k, n = b_at(step)
            eng.wait_ge(b_full[k], b * B_PER + n + 1)
            return banks[4 + k], b_free[k]

        def b_done(eng, b, *steps):
            need = {}
            for step in steps:
                k, n = b_at(step)
                need[k] = max(need.get(k, 0), n + 1)
            for k, n in need.items():
                passed(eng, b_free[k], b * B_PER + n)

        def stand(eng):
            eng.wait_ge(s_setup, 1)

        def y_done(eng, b, l, half):
            if half:
                b_done(eng, b, ("wo", l))
            elif l:
                b_done(eng, b, ("w2", l - 1))
            else:
                a_done(eng, b, "x2T")

        def y_of(l, half):
            return y if l or half else y_in

        block = ctx.enter_context(nc.Block())

        @block.sync
        def _(sp):
            def load(dst, src, s=s_w):
                sp.dma_start(dst, src).then_inc(s, 16)

            def a_load(b):
                sp.dma_start(x_sb[:, b % X_SLOTS], x[b].rearrange("(p j) f -> p j f", j=J)).then_inc(x_loaded, 16)

            load(cols[:], cols_in, s_c)
            load(wmod_sb, wmod, s_c)
            a_load(0)
            load(rows[:], rows_in_.partition_broadcast(P), s_first)
            load(wqkv1_sb[:], wqkv1, s_first)
            load(wqkv_sb[:], wqkv)
            load(wo_sb[:], wo)
            load(w1_sb[:], w1)
            load(w2_sb[:], w2)
            for l in range(L):
                load(rot[:, l], rotary, s_rot)
            sp.wait_ge(s_mask_done, 1)
            load(mask[W:P], mask[0:W], s_mask_both)

            def a_parts(b):
                for n, (scr, parts) in enumerate(((k_scr, (hi, hi, lo, lo)), (v_scr, (hi, lo, hi, lo)))):
                    sp.wait_ge(parts_ready, b * 2 + n + 1)
                    for t, part in enumerate(parts):
                        sp.dma_start(scr[:, :, t].rearrange("q h d s -> (q h) d s"),
                                     part[:, n].rearrange("p j f -> p (j f)").bitcast(F32)).then_inc(parts_out, 16)
                passed(sp, parts_out, b * 16 * 8 + 16 * 8)
                for hh in range(HQ):
                    sp.dma_start(k_rows[32 * hh:32 * hh + 32, hh].bitcast(F32),
                                 k_scr[:, hh].rearrange("q t d s -> (t d) q s")).then_inc(rows_in, 16)
                sp.dma_start(v_rows[:].bitcast(F32), v_scr[:].rearrange("q h t d s -> (h t d) q s")).then_inc(rows_in, 16)

            def b_shift_v(b, l):
                b_done(sp, b, ("kT", l, J - 1))
                sp.dma_start(v_sh[W:P, :, :], v_al[0:W, :, :]).then_inc(v_shifted, 16)
                sp.dma_start(v_sh[0:W, 1:J, :], v_al[W:P, 0:J - 1, :]).then_inc(v_shifted, 16)

            def b_store(b):
                sp.wait_ge(out_ready, b + 1)
                sp.dma_start(out[b].rearrange("(p j) f -> p j f", j=J), gated).then_inc(stored, 16)

            def batch(b, prep=None):
                if prep is not None:
                    stand(sp)
                    passed(sp, stored, 16 * b)
                    a_load(prep)
                for l in range(L):
                    b_shift_v(b, l)
                if prep is not None:
                    a_parts(prep)
                b_store(b)

            sp.wait_ge(x_loaded, 16)
            a_load(1)
            sp.wait_ge(s_zero, 2)
            a_parts(0)
            a_parts(1)
            with sp.Fori(0, B - 2) as b:
                batch(b, b + 2)
            batch(B - 2)
            batch(B - 1)
            passed(sp, stored, 16 * B)

        @block.gpsimd
        def _(pool):
            pool.memset(ident[:], 0.0).then_inc(s_zero, 1)
            pool.wait_ge(s_zero, 1)
            pool.affine_select(out=ident[:], in_=ident[:], compare_op=ALU.not_equal, fill=1.0, base=0,
                               pattern=[[-1, P]], channel_multiplier=1).then_inc(s_ident, 1)
            pool.wait_ge(s_ident, 1)
            pool.tensor_copy(ident_h[:], ident[:]).then_inc(s_ident, 1)
            pool.memset(mask[0:W], 0.0).then_inc(s_mask, 1)
            pool.wait_ge(s_mask, 1)
            pool.affine_select(out=mask[0:W], in_=mask[0:W], compare_op=ALU.is_ge, fill=MASKED, base=0,
                               pattern=[[0, 5], [1, 2 * W]], channel_multiplier=-1).then_inc(s_mask, 1)
            pool.wait_ge(s_mask, 2)
            pool.affine_select(out=mask[0:W], in_=mask[0:W], compare_op=ALU.is_ge, fill=MASKED, base=W,
                               pattern=[[0, 5], [-1, 2 * W]], channel_multiplier=1).then_inc(s_mask, 1)
            pool.wait_ge(s_mask, 3)
            pool.memset(mask[0:W, 0:W], MASKED).then_inc(s_mask_done, 1)
            pool.memset(k_rows[:].bitcast(F32), 0.0).then_inc(s_zero, 1)
            pool.memset(q_bd[:], 0.0).then_inc(s_zero, 1)

            def b_rotary(b, l, n):
                i, w = divmod(n, 2)
                if w:
                    done = (b * L + l) * J + i + 1
                    pool.wait_ge(k_copied, done)
                    v = qk[:, i, 1].rearrange("p (h d) -> p h d", h=H)
                    pool.tensor_tensor(v, v, rot[:, l, i, 1, 0, :].unsqueeze(1).broadcast_to([P, H, DH]),
                                       ALU.mult).then_inc(k_cos, 1)
                    pool.wait_ge(k_cos, done)
                b_done(pool, b, ("qk"[w], l, i))
                pool.tensor_tensor(qk[:, i, w, :], qk[:, i, w, :], sinp[:, n % 2, :], ALU.add).then_inc(rot_sum, 1)

            def b_scale_k(b, l):
                pool.wait_ge(b_chain, b * B_CHAIN + l * (LN_CHAIN + 3) + 3)
                for i in range(J):
                    v = qk[:, i, 1].rearrange("p (h d) -> p h d", h=H)
                    if i == 0:
                        passed(pool, rot_sum, (b * L + l + 1) * 2 * J)
                    pool.tensor_tensor(v, v, rn[:, i, 1, :].unsqueeze(2).broadcast_to([P, H, DH]),
                                       ALU.mult).then_inc(k_ready, 1)

            def b_probs(b, l, u):
                pool.wait_ge(rz2_ready, (b * L + l) * NU + u + 1)
                pool.tensor_tensor(pr[:, u % PR_SLOTS], pr[:, u % PR_SLOTS],
                                   rz2[:, u, :].unsqueeze(2).broadcast_to([P, 4, 2 * W]),
                                   ALU.mult).then_inc(pr_ready, 1)

            with pool.Fori(0, B) as b:
                for l in range(L):
                    for n in range(2 * J):
                        b_rotary(b, l, n)
                    b_scale_k(b, l)
                    for u in range(NU):
                        b_probs(b, l, u)

        @block.scalar
        def _(act):
            act.wait_ge(s_c, 32)
            act.activation(cT[:, 0, :], c_col, ACT.Exp, scale=-1.0).then_inc(s_silexp, 1)

            def a_rsqrt(b):
                act.wait_ge(a_var, b + 1)
                act.activation(logs[:], var_e[:], ACT.Ln).then_inc(a_log, 1)
                act.wait_ge(a_log, b + 1)
                act.activation(rstd0[:], logs[:], ACT.Exp, scale=-0.5).then_inc(a_rstd, 1)

            def a_modulate(b):
                stand(act)
                bank, free = a_see(act, b, "xT")
                act.activation(hT, bank[:].rearrange("p (j n) -> p j n", j=J), ACT.Identity,
                               scale=mod_col[:, b, 0:1], bias=mod_col[:, b, 1:2]).then_inc(free, 1)

            def a_queries(b):
                bank, free = a_see(act, b, "qT")
                act.activation(qT[:], bank[:].rearrange("p (j n) -> p j n", j=J), ACT.Identity,
                               bias=bq_col).then_inc(free, 1)

            def a_exp(b, n):
                g, q = divmod(n, HQ)
                bank, free = a_see(act, b, A_UNITS[n])
                act.wait_ge(max_ready, b * len(A_UNITS) + n + 1)
                if q == 0:
                    passed(act, av_done, b * len(GROUPS) + max(g - E_RING + 1, 0))
                act.activation(E[:, g % E_RING, q, :], bank[:], ACT.Exp, bias=neg_max[:, n:n + 1],
                               accum_out=z[:, n:n + 1]).then_inc(free, 1)

            def b_rsqrt(b, l):
                act.wait_ge(b_var, b * L + l + 1)
                act.activation(logs2[:], var2[:], ACT.Ln).then_inc(b_log, 1)
                act.wait_ge(b_log, b * L + l + 1)
                act.activation(rstd02[:], logs2[:], ACT.Exp, scale=-0.5).then_inc(b_rstd, 1)

            def b_enter_rsqrt(b):
                act.wait_ge(x2_var, b + 1)
                act.activation(logs1[:], var1[:], ACT.Ln).then_inc(x2_log, 1)
                act.wait_ge(x2_log, b + 1)
                act.activation(rstd1[:], logs1[:], ACT.Exp, scale=-0.5).then_inc(x2_rstd, 1)

            def b_enter(b):
                y_rows = y_in[:].rearrange("f (p j) -> f j p", j=J)
                stand(act)
                bank, free = a_see(act, b, "x2T")
                act.activation(y_rows, bank[:].rearrange("p (j n) -> p j n", j=J), ACT.Identity,
                               scale=mod_col[:, b, 2:3], bias=mod_col[:, b, 3:4]).then_inc(free, 1)

            def b_shift(b, l, half):
                y_done(act, b, l, half)
                act.activation(hs[0:W, :], y_of(l, half)[0:W, :], ACT.Copy).then_inc(hs_low, 1)

            def b_square(b, l, n):
                i, w = divmod(n, 2)
                bank, _ = b_see(act, b, ("qk"[w], l, i))
                passed(act, ss_ready, (b * L + l) * 2 * J + max(n - 1, 0))
                act.activation(sq[:, n % 2], bank[:], ACT.Square).then_inc(sq_ready, 1)
                if w:
                    act.activation(qk[:, i, 1, :], bank[:], ACT.Copy).then_inc(k_copied, 1)

            def b_norm(b, l):
                act.wait_ge(ss_all, b * L + l + 1)
                act.activation(nlog[:], ss[:], ACT.Ln).then_inc(ss_log, 1)
                act.wait_ge(ss_log, b * L + l + 1)
                act.activation(rn[:], nlog[:], ACT.Exp, scale=-0.5).then_inc(ss_rsqrt, 1)

            def b_heads(b, l, i):
                bank, _ = b_see(act, b, ("qT", l, i))
                act.activation(q_bd[0:W, :, 2 * i:2 * i + 2, 0, :],
                               bank[:].rearrange("p (c w t) -> p c w t", c=PAIRS, w=2)[0:W],
                               ACT.Copy).then_inc(q_low, 1)
                bank, free = b_see(act, b, ("kT", l, i))
                act.activation(kT[:, :, W + P * i:W + P * i + P], bank[:].rearrange("p (c t) -> p c t", c=PAIRS),
                               ACT.Copy).then_inc(free, 1)

            def b_values(b, l, i):
                bank, free = b_see(act, b, ("v", l, i))
                act.activation(v_al[:, i, :], bank[:], ACT.Copy).then_inc(free, 1)

            def b_exp(b, l, u):
                bank, free = b_see(act, b, ("sim", l, u))
                act.wait_ge(max2, (b * L + l) * NU + u + 1)
                if u >= PR_SLOTS:
                    b_see(act, b, ("pT", l, u - PR_SLOTS))
                for w in range(4):
                    last = act.activation(pr[:, u % PR_SLOTS, w, :], bank[:, 2 * W * w:2 * W * (w + 1)], ACT.Exp,
                                          bias=neg2[:, u, w:w + 1], accum_out=z2[:, u, w:w + 1])
                last.then_inc(free, 1)

            def b_probsT(b, l, u):
                bank, free = b_see(act, b, ("pT", l, u))
                if l == 0 and u == 0:
                    passed(act, stored, 16 * b)
                if u >= 2:
                    b_see(act, b, ("av", l, u - 2))
                act.activation(prT[:, u % 2], bank[:].rearrange("p (w n) -> p w n", w=4), ACT.Copy).then_inc(free, 1)

            def b_ln(b, l):
                bank, free = b_see(act, b, ("lnT", l))
                act.activation(h2T, bank[:], ACT.Identity, scale=lng_col[l], bias=lnb_col[l]).then_inc(free, 1)

            def b_gelu(b, l, k):
                bank, free = b_see(act, b, ("gate", l, k))
                act.activation(gel[k][0:CH[k]], bank[0:CH[k]], ACT.Gelu,
                               bias=b1_col[l][1][k]).then_inc(free, 1)

            def a_units(b, *place):
                for n in units_after(*place) if b is not None else ():
                    a_exp(b, n)

            def batch(b, nxt=None, prep=None):
                act.preload_act_table_set(EXP_LN)
                for l in range(L):
                    if l:
                        b_shift(b, l, 0)
                    a_units(nxt, "shift", l)
                    for n in range(2 * J):
                        b_square(b, l, n)
                        if n % 2:
                            b_values(b, l, n // 2)
                        a_units(nxt, "rotate", l, n)
                    b_norm(b, l)
                    a_units(nxt, "norm", l)
                    for i in range(J):
                        b_heads(b, l, i)
                        a_units(nxt, "heads", l, i)
                    if l == L - 1 and prep is not None:
                        a_rsqrt(prep)
                    for u in range(NU + PT_LAG):
                        if u < NU:
                            b_exp(b, l, u)
                        a_units(nxt, "scores", l, u)
                        if u >= PT_LAG:
                            b_probsT(b, l, u - PT_LAG)
                        a_units(nxt, "values", l, u)
                    a_units(nxt, "wo", l)
                    if l == L - 1 and nxt is not None:
                        b_enter_rsqrt(nxt)
                    b_shift(b, l, 1)
                    if l == L - 1 and nxt is not None:
                        b_enter(nxt)
                    b_rsqrt(b, l)
                    a_units(nxt, "ln", l)
                    b_ln(b, l)
                    if l == L - 1 and prep is not None:
                        a_modulate(prep)
                    for k in range(3):
                        b_gelu(b, l, k)
                    if l < L - 1:
                        act.preload_act_table_set(EXP_LN)
                    a_units(nxt, "up", l)
                if prep is not None:
                    a_queries(prep)
                if nxt is not None:
                    b_shift(nxt, 0, 0)

            act.preload_act_table_set(EXP_LN)
            a_rsqrt(0)
            act.wait_ge(s_setup, 1)
            a_modulate(0)
            a_queries(0)
            for n in range(len(A_UNITS)):
                a_exp(0, n)
            a_rsqrt(1)
            b_enter_rsqrt(0)
            b_enter(0)
            a_modulate(1)
            a_queries(1)
            b_shift(0, 0, 0)
            with act.Fori(0, B - 2) as b:
                batch(b, b + 1, b + 2)
            batch(B - 2, B - 1)
            batch(B - 1)

        @block.vector
        def _(dve):
            def chained(s, per):
                state = [0, 0]

                def start(b):
                    state[:] = [b * per, 0]

                def link(ins):
                    state[1] += 1
                    ins.then_inc(s, 1)
                    dve.wait_ge(s, state[0] + state[1])

                def end():
                    assert state[1] == per, state
                return start, link, end

            s_start, s_link, _ = chained(s_chain, 0)
            ln_start, ln_link, ln_end = chained(ln_chain, LN_CHAIN)
            split_start, split_link, split_end = chained(split_chain, 2)
            a_start, a_link, a_end = chained(a_chain, len(GROUPS))
            enter_start, enter_link, enter_end = chained(enter_chain, LN_CHAIN)
            b_start, b_link, b_end = chained(b_chain, B_CHAIN)

            for s in credited:
                dve.sem_inc(s, 1)
            s_start(0)
            s_link(dve.memset(qz[:], 0.0))
            s_link(dve.memset(kT[:, :, 0:W], 0.0))
            s_link(dve.memset(hs[W:P, 0:1], 0.0))

            def silu():
                dve.wait_ge(s_silexp, 1)
                s_link(dve.tensor_scalar(cT[:, 0, :], cT[:, 0, :], 1.0, None, ALU.add))
                s_link(dve.reciprocal(cT[:, 1, :], cT[:, 0, :]))
                dve.tensor_tensor(cT[:, 0, :], c_col, cT[:, 1, :], ALU.mult).then_inc(s_sil, 1)

            def modulation():
                dve.wait_ge(s_mod, 1)
                m = O_BANK[:, 0:4 * B].rearrange("p (m b) -> p m b", m=4)
                s_link(dve.tensor_scalar(mod_col[:, :, 0], m[:, 0], 1.0, None, ALU.add))
                s_link(dve.tensor_copy(mod_col[:, :, 1], m[:, 1]))
                s_link(dve.tensor_scalar(mod_col[:, :, 2], m[:, 2], 1.0, None, ALU.add))
                s_link(dve.tensor_copy(mod_col[:, :, 3], m[:, 3]))
                dve.wait_ge(s_first, 16 * 2)
                dve.tensor_scalar(bk_bc, bk_bc, temp_col, None, ALU.mult).then_inc(s_setup, 1)
                dve.wait_ge(s_setup, 1)

            def gates():
                dve.wait_ge(s_gates, 1)
                for n in range(4):
                    s_link(dve.tensor_copy(gate_bc[:, :, 2 * n:2 * n + 2, :],
                                           banks[4 + n][:].rearrange("p (b g f) -> p g b f", b=2, g=2)))
                raw = gate_bc[:].rearrange("p g b f -> p (g b f)")
                sign = rot_work[:].rearrange("p n f -> p (n f)")
                size = work[:, J * INNER:]
                s_link(dve.tensor_scalar(sign, raw, 0.0, 2.0, ALU.is_ge, ALU.mult))
                s_link(dve.scalar_tensor_tensor(size, raw, -1.0, raw, ALU.mult, ALU.max))
                s_link(dve.tensor_scalar(size, size, 0.25, None, ALU.max))
                s_link(dve.scalar_tensor_tensor(raw, sign, -1.0, size, ALU.add, ALU.mult))

            def tables():
                dve.wait_ge(s_rot, 16 * L)
                dve.wait_ge(s_zero, 3)
                for l in range(L):
                    for w in range(2):
                        sc = scale_bc[:, l, w, :]
                        s_link(dve.tensor_tensor(rot[:, l, :, w, 0, :], rot[:, l, :, w, 0, :],
                                                 sc.unsqueeze(1).broadcast_to([P, J, DH]), ALU.mult))
                        for a in range(2):
                            r = rot[:, l, :, w, 1, 32 * a:32 * a + 32]
                            s_link(dve.tensor_tensor(r, r, sc[:, 32 - 32 * a:64 - 32 * a].unsqueeze(1)
                                                     .broadcast_to([P, J, 32]), ALU.mult))

            def var_of(src, stats, mv, var, link, ready):
                for j in range(J):
                    last = dve.bn_stats(stats[:, j, :], src[:, j, :])
                link(last)
                dve.tensor_copy(var, stats[:, :, 0])
                for j in range(J):
                    last = dve.bn_aggr(mv[:, j, :], stats[:, j, :])
                link(last)
                dve.tensor_scalar(var, mv[:, :, 1], LN_EPS, None, ALU.add).then_inc(ready, 1)

            def newton(v, r, t, link):
                link(dve.scalar_tensor_tensor(t, v, -0.5, r, ALU.mult, ALU.mult))
                link(dve.tensor_tensor(t, t, r, ALU.mult))
                link(dve.scalar_tensor_tensor(r, t, 1.5, r, ALU.add, ALU.mult))

            def normalize(dst, src, mv, rstd):
                for j in range(J):
                    last = dve.tensor_scalar(dst[:, j, :], src[:, j, :], mv[:, j, 0:1], rstd[:, j:j + 1],
                                             ALU.subtract, ALU.mult)
                return last

            def a_var_of(b):
                ln_start(b)
                if not isinstance(b, int):
                    stand(dve)
                dve.wait_ge(x_loaded, 16 * b + 16)
                var_of(x_sb[:, b % X_SLOTS], stats, mv, var_e[:], ln_link, a_var)

            def a_normalize(b):
                dve.wait_ge(a_rstd, b + 1)
                newton(var_e[:], rstd0[:], tmp4[:], ln_link)
                normalize(xn, x_sb[:, b % X_SLOTS], mv, rstd0).then_inc(xn_ready, 1)
                ln_end()

            def a_split(b):
                split_start(b)
                for n, step in enumerate("kv"):
                    bank, free = a_see(dve, b, step)
                    src = bank[:].rearrange("p (j f) -> p j f", j=J)
                    if n == 0:
                        passed(dve, parts_out, b * 16 * 8)
                        dve.scalar_tensor_tensor(kf[:, n], src, temp_col,
                                                 bk_bc.unsqueeze(1).broadcast_to([P, J, D]),
                                                 ALU.mult, ALU.add).then_inc(free, 1)
                    else:
                        dve.tensor_tensor(kf[:, n], src, bv_bc.unsqueeze(1).broadcast_to([P, J, D]),
                                          ALU.add).then_inc(free, 1)
                    a_done(dve, b, step)
                    split_link(dve.tensor_copy(hi[:, n], kf[:, n]))
                    dve.tensor_tensor(lo[:, n], kf[:, n], hi[:, n].bitcast(F32), ALU.subtract).then_inc(parts_ready, 1)
                split_end()

            def a_max(b, n):
                bank, _ = a_see(dve, b, A_UNITS[n])
                dve.tensor_reduce(neg_max[:, n:n + 1], bank[:], AX.X, ALU.max, negate=True).then_inc(max_ready, 1)

            def a_weigh(b, g):
                hh, j = GROUPS[g]
                a_done(dve, b, A_UNITS[HQ * g + HQ - 1])
                a_link(dve.reciprocal(rz[:, HQ * (g % 2):HQ * (g % 2) + HQ], z[:, HQ * g:HQ * g + HQ]))
                if g == 0:
                    a_done(dve, b, "qT")
                if j >= QZ_SLOTS:
                    passed(dve, av_done, b * len(GROUPS) + g - QZ_SLOTS + 1)
                dve.tensor_tensor(qz[:, hh, j % QZ_SLOTS, :, DA * hh:DA * hh + DA],
                                  qT[:, j, :].rearrange("p (q h d) -> p q h d", q=HQ, h=HQ)[:, :, hh, :],
                                  rz[:, HQ * (g % 2):HQ * (g % 2) + HQ].unsqueeze(2).broadcast_to([P, HQ, DA]),
                                  ALU.mult).then_inc(qz_ready, 1)

            def a_residual(b):
                passed(dve, av_done, b * len(GROUPS) + len(GROUPS))
                dve.tensor_tensor(xn, O_BANK[:].rearrange("p (j f) -> p j f", j=J),
                                  gate_bc[:, 0, b, :].unsqueeze(1).broadcast_to([P, J, D]),
                                  ALU.mult).then_inc(o_read, 1)
                passed(dve, o_read, b + 1)
                xb = x_sb[:, b % X_SLOTS]
                dve.tensor_tensor(xb, xb, xn, ALU.add).then_inc(x2_ready, 1)
                a_end()

            def b_enter_var(b):
                enter_start(b)
                stand(dve)
                dve.wait_ge(x2_ready, b + 1)
                var_of(x_sb[:, b % X_SLOTS], stats1, mv1, var1[:], enter_link, x2_var)

            def b_enter_normalize(b):
                dve.wait_ge(x2_rstd, b + 1)
                newton(var1[:], rstd1[:], tmp1[:], enter_link)
                normalize(xn2, x_sb[:, b % X_SLOTS], mv1, rstd1).then_inc(xn2_ready, 1)
                enter_end()

            def b_shift(b, l, half):
                y_done(dve, b, l, half)
                dve.tensor_copy(hs[W:P, 1:T], y_of(l, half)[W:P, 0:T - 1]).then_inc(hs_up, 1)

            def b_rotate(b, l, n):
                i, w = divmod(n, 2)
                k = (b * L + l) * 2 * J + n
                if w:
                    dve.wait_ge(k_copied, (b * L + l) * J + i + 1)
                    bank, free = b_see(dve, b, ("k", l, i))
                else:
                    dve.wait_ge(sq_ready, k + 1)
                    bank, free = b_see(dve, b, ("q", l, i))
                    dve.tensor_tensor(qk[:, i, 0, :].rearrange("p (h d) -> p h d", h=H),
                                      bank[:].rearrange("p (h d) -> p h d", h=H),
                                      rot[:, l, i, 0, 0, :].unsqueeze(1).broadcast_to([P, H, DH]), ALU.mult)
                passed(dve, rot_sum, (b * L + l) * 2 * J + max(n - 1, 0))
                dve.tensor_tensor(sinp[:, n % 2, :].rearrange("p (h a r) -> p h a r", h=H, a=2),
                                  bank[:].rearrange("p (h a r) -> p h a r", h=H, a=2)[:, :, ::-1, :],
                                  rot[:, l, i, w, 1, :].rearrange("p (a r) -> p a r", a=2).unsqueeze(1)
                                  .broadcast_to([P, H, 2, 32]), ALU.mult).then_inc(free, 1)
                dve.tensor_reduce(ss[:, i, w, :], sq[:, n % 2, :].rearrange("p (h d) -> p h d", h=H),
                                  AX.X, ALU.add).then_inc(ss_ready, 1)

            def b_norm(b, l):
                passed(dve, ss_ready, (b * L + l + 1) * 2 * J)
                dve.tensor_scalar(ss[:], ss[:], NORM_MIN2, SHIFT2, ALU.max, ALU.mult).then_inc(ss_all, 1)

            def b_scale(b, l):
                dve.wait_ge(ss_rsqrt, b * L + l + 1)
                newton(ss[:], rn[:], nt[:], b_link)
                for i in range(J):
                    passed(dve, rot_sum, (b * L + l) * 2 * J + 2 * i + 1)
                    v = qk[:, i, 0].rearrange("p (h d) -> p h d", h=H)
                    dve.tensor_tensor(v, v, rn[:, i, 0, :].unsqueeze(2).broadcast_to([P, H, DH]),
                                      ALU.mult).then_inc(q_ready, 1)

            def b_heads(b, l, i):
                bank, free = b_see(dve, b, ("qT", l, i))
                dve.wait_ge(q_low, (b * L + l) * J + i + 1)
                dve.tensor_copy(q_bd[W:P, :, 2 * i:2 * i + 2, 1, :],
                                bank[:].rearrange("p (c w t) -> p c w t", c=PAIRS, w=2)[W:P]).then_inc(free, 1)

            def b_pad_v(b, l):
                b_see(dve, b, ("kT", l, J - 1))
                dve.memset(v_sh[0:W, 0, :], 0.0).then_inc(v_pad, 1)

            def b_max(b, l, u):
                bank, _ = b_see(dve, b, ("sim", l, u))
                dve.tensor_reduce(neg2[:, u, :], bank[:].rearrange("p (w n) -> p w n", w=4), AX.X, ALU.max,
                                  negate=True).then_inc(max2, 1)

            def b_sums(b, l, u):
                b_done(dve, b, ("sim", l, u))
                dve.reciprocal(rz2[:, u, :], z2[:, u, :]).then_inc(rz2_ready, 1)

            def b_heads_out(b, l, u):
                p, g = AT_UNITS[u]
                bank, free = b_see(dve, b, ("av", l, u))
                src = bank[:].rearrange("p (w h t) -> p w h t", w=4, h=2)
                dst = oT[:, p, 4 * W * g:4 * W * (g + 1)].rearrange("p (w t) -> p w t", w=4)
                dve.tensor_copy(dst[0:W], src[0:W, :, 0, :])
                dve.tensor_copy(dst[W:P], src[W:P, :, 1, :]).then_inc(free, 1)

            def b_residual(b, l):
                bank, free = b_see(dve, b, ("wo", l))
                y_read(dve, b, l, 0)
                dve.tensor_tensor(y[:], bank[:], y_of(l, 0)[:], ALU.add).then_inc(free, 1)

            def y_read(dve, b, l, half):
                dve.wait_ge(hs_low, (b * L + l) * 2 + half + 1)
                dve.wait_ge(hs_up, (b * L + l) * 2 + half + 1)

            def b_ln_var(b, l):
                stand(dve)
                bank, _ = b_see(dve, b, ("tok", l))
                var_of(bank[:].rearrange("p (j f) -> p j f", j=J), stats2, mv2, var2[:], b_link, b_var)

            def b_ln(b, l):
                bank, free = b_see(dve, b, ("tok", l))
                src = bank[:].rearrange("p (j f) -> p j f", j=J)
                dve.wait_ge(b_rstd, b * L + l + 1)
                newton(var2[:], rstd02[:], tmp2[:], b_link)
                normalize(hn, src, mv2, rstd02).then_inc(free, 1)

            def b_up(b, l, k):
                bank, free = b_see(dve, b, ("up", l, k))
                b_done(dve, b, ("gate", l, k))
                dve.scalar_tensor_tensor(up[k][0:CH[k]], bank[0:CH[k]], b1_col[l][0][k],
                                         gel[k][0:CH[k]], ALU.add, ALU.mult).then_inc(free, 1)

            def b_down(b, l):
                bank, free = b_see(dve, b, ("w2", l))
                y_read(dve, b, l, 1)
                dve.scalar_tensor_tensor(y[:], bank[:], b2_col[l], y[:], ALU.add, ALU.add).then_inc(free, 1)

            def b_out(b):
                for j in range(J):
                    bank, free = b_see(dve, b, ("yT", j))
                    dve.tensor_tensor(gated[:, j], bank[:, 0:P], gate_bc[:, 1, b, :], ALU.mult).then_inc(free, 1)
                b_done(dve, b, *(("yT", j) for j in range(J)))
                dve.tensor_tensor(gated, gated, x_sb[:, b % X_SLOTS], ALU.add).then_inc(out_ready, 1)
                b_end()

            def a_unit(b, n):
                if n == 0:
                    a_start(b)
                if n < len(A_UNITS):
                    a_max(b, n)
                if n >= HQ - 1 + LAG - 1 and (n - (HQ - 1 + LAG - 1)) % HQ == 0:
                    a_weigh(b, (n - (HQ - 1 + LAG - 1)) // HQ)

            def a_units(b, *place):
                for n in units_after(*place) if b is not None else ():
                    a_unit(b, n)

            def a_finish(b):
                for n in range(len(A_UNITS), len(A_UNITS) + LAG):
                    a_unit(b, n)

            def batch(b, nxt=None, prep=None):
                b_start(b)
                for l in range(L):
                    if l:
                        b_shift(b, l, 0)
                    a_units(nxt, "shift", l)
                    for n in range(2 * J):
                        b_rotate(b, l, n)
                        a_units(nxt, "rotate", l, n)
                    b_norm(b, l)
                    a_units(nxt, "norm", l)
                    b_scale(b, l)
                    for i in range(J):
                        a_units(nxt, "heads", l, i)
                        b_heads(b, l, i)
                    b_pad_v(b, l)
                    if l == L - 1 and prep is not None:
                        a_var_of(prep)
                    for u in range(NU + AV_LAG):
                        if u < NU:
                            b_max(b, l, u)
                        a_units(nxt, "scores", l, u)
                        if 1 <= u <= NU:
                            b_sums(b, l, u - 1)
                        if u >= AV_LAG:
                            b_heads_out(b, l, u - AV_LAG)
                        a_units(nxt, "values", l, u)
                        if l == L - 1 and u == NU and nxt is not None:
                            a_finish(nxt)
                    if l == L - 1 and nxt is not None:
                        a_residual(nxt)
                        b_enter_var(nxt)
                    a_units(nxt, "wo", l)
                    b_residual(b, l)
                    b_shift(b, l, 1)
                    if l == L - 1 and nxt is not None:
                        b_enter_normalize(nxt)
                    b_ln_var(b, l)
                    a_units(nxt, "ln", l)
                    b_ln(b, l)
                    if l == L - 1 and prep is not None:
                        a_normalize(prep)
                    if l == L - 1 and nxt is not None:
                        b_shift(nxt, 0, 0)
                    for k in range(3):
                        b_up(b, l, k)
                    if l == L - 1 and prep is not None:
                        a_split(prep)
                    a_units(nxt, "up", l)
                    b_down(b, l)
                b_out(b)

            silu()
            a_var_of(0)
            a_normalize(0)
            modulation()
            a_split(0)
            gates()
            tables()
            for n in range(len(A_UNITS)):
                a_unit(0, n)
            a_var_of(1)
            a_finish(0)
            a_residual(0)
            b_enter_var(0)
            b_enter_normalize(0)
            a_normalize(1)
            b_shift(0, 0, 0)
            a_split(1)
            with dve.Fori(0, B - 2) as b:
                batch(b, b + 1, b + 2)
            batch(B - 2, B - 1)
            batch(B - 1)

        @block.tensor
        def _(pe):
            pe.wait_ge(s_c, 32)
            pe.wait_ge(s_sil, 1)
            sil = cT[:, 0, :]
            for n, m in enumerate((1, 0, 4, 3)):
                last = pe.matmul(O_BANK[:, B * n:B * (n + 1)], wmod_sb[:, D * m:D * (m + 1)], sil, start=True, stop=True)
            last.then_inc(s_mod, 1)

            def gate_rows():
                for b in range(B):
                    for n, m in enumerate((2, 5)):
                        o = (b % 2) * 2 * D + n * D
                        last = pe.matmul(banks[4 + b // 2][:, o:o + D], sil[:, b:b + 1].broadcast_to([D, P]),
                                         wmod_sb[:, D * m:D * (m + 1)], start=True, stop=True)
                last.then_inc(s_gates, 1)

            def a_transpose(b):
                pe.wait_ge(xn_ready, b + 1)
                bank, full = a_take(pe, b, "xT")
                for j in range(J):
                    last = pe.transpose(bank[:, P * j:P * (j + 1)], xn[:, j, :], ident[:])
                last.then_inc(full, 1)

            def a_project(b):
                a_done(pe, b, "xT")
                bank, full = a_take(pe, b, "qT")
                pe.matmul(bank[:], wq_sb, E[:, 0, 2, :], start=True, stop=True).then_inc(full, 1)
                for step, w in (("k", wk_sb), ("v", wv_sb)):
                    bank, full = a_take(pe, b, step)
                    for j in range(J):
                        last = pe.matmul(bank[:, D * j:D * (j + 1)], hT[:, j, :], w, start=True, stop=True)
                    last.then_inc(full, 1)

            def a_scores(b, n):
                hh, j, q = A_UNITS[n]
                if n == 0:
                    passed(pe, rows_in, (b + 1) * 16 * (HQ + 1))
                bank, full = a_take(pe, b, A_UNITS[n])
                pe.matmul(bank[:], k_rows[:, hh, q, P * j:P * (j + 1)], v_rows[:, q, :],
                          start=True, stop=True).then_inc(full, 1)

            def a_values(b, g):
                hh, j = GROUPS[g]
                pe.wait_ge(qz_ready, b * len(GROUPS) + g + 1)
                if g == 0:
                    passed(pe, o_read, b)
                for q in range(HQ):
                    last = pe.matmul(O_BANK[32 * q:32 * q + 32, :], qz[:, hh, j % QZ_SLOTS, q, :], E[:, g % E_RING, q, :],
                                     start=(g == 0), stop=(g == len(GROUPS) - 1))
                last.then_inc(av_done, 1)

            def b_enter(b):
                pe.wait_ge(xn2_ready, b + 1)
                bank, full = a_take(pe, b, "x2T")
                for j in range(J):
                    last = pe.transpose(bank[:, P * j:P * (j + 1)], xn2[:, j, :], ident[:])
                last.then_inc(full, 1)

            def hs_wait(b, l, half):
                pe.wait_ge(hs_low, (b * L + l) * 2 + half + 1)
                pe.wait_ge(hs_up, (b * L + l) * 2 + half + 1)

            def b_project(b, l, i, w):
                bank, full = b_take(pe, b, ("qkv"[w], l, i))
                pe.matmul(bank[:], hs[:, P * i:P * (i + 1)], wqkv_sb[:, l, INNER * w:INNER * (w + 1)],
                          start=True, stop=True).then_inc(full, 1)

            def b_heads(b, l, i):
                for w in range(2):
                    pe.wait_ge((q_ready, k_ready)[w], (b * L + l) * J + i + 1)
                    bank, full = b_take(pe, b, (("qT", "kT")[w], l, i))
                    for p in range(PAIRS):
                        last = pe.transpose(bank[:, P * p:P * (p + 1)], qk[:, i, w, P * p:P * (p + 1)], ident[:])
                    last.then_inc(full, 1)

            def b_scores(b, l, u):
                p, g = AT_UNITS[u]
                tiles = [(s, l, 2 * g + i) for s in ("qT", "kT") for i in range(2)] if u < 2 else []
                bank, full = b_take(pe, b, ("sim", l, u), *tiles)
                pe.matmul(bank[:], ident_h[:], mask[:, 2 * W * g:2 * W * (g + 4)],
                          start=True, stop=False)
                for w in range(4):
                    n = 4 * g + w
                    last = pe.matmul(bank[:, 2 * W * w:2 * W * (w + 1)], q_bd[:, p, n].rearrange("p h t -> p (h t)"),
                                     kT[:, p, W * n:W * n + 2 * W], start=False, stop=(w == 3))
                last.then_inc(full, 1)

            def b_probsT(b, l, u):
                pe.wait_ge(pr_ready, (b * L + l) * NU + u + 1)
                bank, full = b_take(pe, b, ("pT", l, u))
                for w in range(4):
                    last = pe.transpose(bank[:, P * w:P * (w + 1)], pr[:, u % PR_SLOTS, w, :], ident[:])
                last.then_inc(full, 1)

            def b_values(b, l, u):
                p, g = AT_UNITS[u]
                if u == 0:
                    pe.wait_ge(v_shifted, (b * L + l + 1) * 32)
                    pe.wait_ge(v_pad, b * L + l + 1)
                bank, full = b_take(pe, b, ("av", l, u), ("pT", l, u))
                for w in range(4):
                    n = 4 * g + w
                    v = v_al[:, n // 2] if n % 2 else v_sh[:, n // 2]
                    last = pe.matmul(bank[:, P * w:P * (w + 1)], v[:, P * p:P * (p + 1)], prT[:, u % 2, w, :],
                                     start=True, stop=True)
                last.then_inc(full, 1)

            def b_project_out(b, l):
                bank, full = b_take(pe, b, ("wo", l))
                for p in range(PAIRS):
                    b_done(pe, b, *(("av", l, u) for u in range(NU) if AT_UNITS[u][0] == p))
                    last = pe.matmul(bank[:], wo_sb[:, l, p, :], oT[:, p, :], start=(p == 0), stop=(p == PAIRS - 1))
                last.then_inc(full, 1)

            def b_ln_in(b, l):
                hs_wait(b, l, 1)
                bank, full = b_take(pe, b, ("tok", l))
                for i in range(J):
                    last = pe.transpose(bank[:, P * i:P * (i + 1)], hs[:, P * i:P * (i + 1)], ident[:])
                last.then_inc(full, 1)

            def b_ln_out(b, l):
                bank, full = b_take(pe, b, ("lnT", l), ("tok", l))
                for i in range(J):
                    last = pe.transpose(bank[:, P * i:P * (i + 1)], hn[:, i, :], ident[:])
                last.then_inc(full, 1)

            def b_hidden(b, l, k, a):
                bank, full = b_take(pe, b, (("up", "gate")[a], l, k), ("lnT", l))
                o = a * HID + P * k
                pe.matmul(bank[0:CH[k]], w1_sb[:, l, o:o + CH[k]], h2T, start=True, stop=True).then_inc(full, 1)

            def b_down(b, l):
                bank, full = b_take(pe, b, ("w2", l))
                for k in range(3):
                    b_done(pe, b, ("up", l, k))
                    last = pe.matmul(bank[:], w2_sb[0:CH[k], l, k, :], up[k][0:CH[k]], start=(k == 0), stop=(k == 2))
                last.then_inc(full, 1)

            def b_leave(b):
                y_rows = y[:].rearrange("f (p j) -> f j p", j=J)
                for j in range(J):
                    bank, full = b_take(pe, b, ("yT", j), ("w2", L - 1))
                    pe.transpose(bank[:, 0:P], y_rows[:, j, :], ident[:]).then_inc(full, 1)

            def a_unit(b, n):
                if n + LEAD < len(A_UNITS):
                    a_scores(b, n + LEAD)
                if n >= HQ - 1 + LAG and (n - (HQ - 1 + LAG)) % HQ == 0:
                    a_values(b, (n - (HQ - 1 + LAG)) // HQ)

            def a_units(b, *place):
                for n in units_after(*place) if b is not None else ():
                    if n == 0:
                        a_begin(b)
                    a_unit(b, n)

            def a_begin(b):
                for n in range(LEAD):
                    a_scores(b, n)

            def a_finish(b):
                for n in range(len(A_UNITS), len(A_UNITS) + LAG):
                    a_unit(b, n)

            def batch(b, nxt=None, prep=None):
                for l in range(L):
                    a_units(nxt, "shift", l)
                    hs_wait(b, l, 0)
                    for i in range(J):
                        for w in range(3):
                            b_project(b, l, i, w)
                            if w < 2:
                                a_units(nxt, "rotate", l, 2 * i + w)
                    a_units(nxt, "norm", l)
                    for i in range(J):
                        b_heads(b, l, i)
                        a_units(nxt, "heads", l, i)
                    for u in range(NU + AV_LAG):
                        if u < NU:
                            b_scores(b, l, u)
                        a_units(nxt, "scores", l, u)
                        if PT_LAG <= u < NU + PT_LAG:
                            b_probsT(b, l, u - PT_LAG)
                        if u >= AV_LAG:
                            b_values(b, l, u - AV_LAG)
                        a_units(nxt, "values", l, u)
                        if l == L - 1 and u == NU and nxt is not None:
                            a_finish(nxt)
                    a_units(nxt, "wo", l)
                    b_project_out(b, l)
                    if l == L - 1 and nxt is not None:
                        b_enter(nxt)
                    b_ln_in(b, l)
                    a_units(nxt, "ln", l)
                    b_ln_out(b, l)
                    if l == L - 1 and prep is not None:
                        a_transpose(prep)
                    for k in range(3):
                        b_hidden(b, l, k, 1)
                    for k in range(3):
                        b_hidden(b, l, k, 0)
                    if l == L - 1 and prep is not None:
                        a_project(prep)
                    a_units(nxt, "up", l)
                    b_down(b, l)
                b_leave(b)

            pe.wait_ge(s_ident, 2)
            a_transpose(0)
            pe.wait_ge(s_setup, 1)
            pe.wait_ge(s_first, 16 * 2)
            a_project(0)
            gate_rows()
            a_begin(0)
            for n in range(len(A_UNITS)):
                a_unit(0, n)
            a_finish(0)
            pe.wait_ge(s_w, 16 * N_W)
            pe.wait_ge(s_mask_both, 16)
            b_enter(0)
            a_transpose(1)
            a_project(1)
            with pe.Fori(0, B - 2) as b:
                batch(b, b + 1, b + 2)
            batch(B - 2, B - 1)
            batch(B - 1)


def laid_out(inputs):
    a = {n[3:]: np.asarray(v) for n, v in inputs.items()}
    cols = np.zeros((P, N_COLS), np.float32)
    cols[:, 0] = a["attn_bq"]
    cols[:, 1] = np.repeat(a["attn_temperature"].reshape(-1), DA)
    for l in range(L):
        cols[:, 2 + l] = a["ffn_b2"][l]
        cols[:, 2 + L + l] = a["ffn_ln_g"][l]
        cols[:, 2 + 2 * L + l] = a["ffn_ln_b"][l]
        for h in range(2):
            for k in range(3):
                cols[:CH[k], 2 + 3 * L + (l * 2 + h) * 3 + k] = a["ffn_b1"][l, h * HID + P * k:][:CH[k]]
    cols[:, N_COLS - B:] = a["c"].T
    w2 = np.zeros((L, 3 * P, D), np.float32)
    w2[:, :HID] = a["ffn_w2"]
    return {
        "x": a["attn_x"], "wmod": a["wmod"],
        "wqkv1": np.stack([a["attn_Wq"], a["attn_Wk"], a["attn_Wv"]], 1),
        "wqkv": a["ffn_wqkv"].transpose(1, 0, 2),
        "wo": a["ffn_wo"].reshape(L, PAIRS, P, D).transpose(2, 0, 1, 3),
        "w1": a["ffn_w1"].transpose(1, 0, 2),
        "w2": w2.reshape(L, 3, P, D).transpose(2, 0, 1, 3),
        "cols": cols,
        "rows": np.concatenate([a["attn_bk"], a["attn_bv"], a["ffn_q_scale"].reshape(-1), a["ffn_k_scale"].reshape(-1)]),
        "rotary": rotary_tables(),
    }


def rotary_tables():
    half = np.arange(0, DH, 2, dtype=np.float32)
    inv = (np.float32(1.0) / np.float32(10000.0) ** (half / np.float32(DH))).astype(np.float32)
    t = np.arange(T, dtype=np.float32)
    freqs = t[:, None] * inv[None, :]
    freqs = np.concatenate([freqs, freqs], -1).astype(np.float64)
    base = (half + np.float32(0.4 * DH)) / np.float32(1.4 * DH)
    power = (t - T // 2) / np.float32(W // 2)
    scale = base[None, :].astype(np.float32) ** power[:, None]
    scale = np.concatenate([scale, scale], -1).astype(np.float64)
    sign = np.where(np.arange(DH) < DH // 2, -1.0, 1.0)
    cos, sin = np.cos(freqs), np.sin(freqs) * sign
    q = np.stack([cos * scale, sin * scale], 1) * 8.0 * 1024.0
    k = np.stack([cos / scale, sin / scale], 1) * 1024.0
    tab = np.stack([q, k], 1).astype(np.float32)
    return np.ascontiguousarray(tab.reshape(J, P, 2, 2, DH).transpose(1, 0, 2, 3, 4))


def kernel(**inputs):
    import concourse.bacc as _bacc
    from concourse.bass_utils import run_bass_kernel_spmd as _run

    nc = _bacc.Bacc("TRN2", target_bir_lowering=False, num_devices=1)
    arrays, args = {}, []
    for name, a in laid_out(inputs).items():
        a = np.ascontiguousarray(a)
        arrays[f"in_{name}"] = a
        args.append(nc.dram_tensor(f"in_{name}", a.shape, mybir.dt.from_np(a.dtype), kind="ExternalInput").ap())
    out = nc.dram_tensor("out", (B, T, D), F32, kind="ExternalOutput").ap()
    build(nc, *args, out)
    r = _run(nc, [arrays], core_ids=[0])
    return r.results[0]["out"]
```
